# Optimizing a Trainium2 kernel written in Bass

```python
import numpy as np
import jax
import jax.numpy as jnp

def _softmax(x, axis=-1):
    return jax.nn.softmax(x, axis=axis)

def _gelu(x):
    return jax.nn.gelu(x, approximate=True)

def _silu(x):
    return jax.nn.silu(x)

def _sigmoid(x):
    return jax.nn.sigmoid(x)

def _layernorm(x, axis=-1, eps=1e-05):
    m = jnp.mean(x, axis=axis, keepdims=True)
    v = jnp.var(x, axis=axis, keepdims=True)
    return (x - m) / jnp.sqrt(v + eps)

def _scatter_add(tgt, idx, src, axis=0):
    return tgt.at[idx].add(src)

def _segment_sum(src, seg, n):
    return jax.ops.segment_sum(src, seg, n)
kernel_name = 'mk_xattn_ffn_d1_seqx_r4_4917d7'

def setup_inputs(seed: int=0):
    np.random.seed(seed)
    _w = jnp.asarray

    def _rec_inputs():
        import jax
        import jax.numpy as jnp
        _rk = jax.random.key(seed)
        x = 7.22e-05 + 1 * jax.random.normal(jax.random.fold_in(_rk, 1), (16, 256, 256), jnp.float32)
        _lenS = 256 - jax.random.randint(jax.random.fold_in(_rk, 7), (16,), 0, max(1, 256 // 4) + 1, jnp.int32)
        _lenS2 = 256 - jax.random.randint(jax.random.fold_in(_rk, 8), (16,), 0, max(1, 256 // 4) + 1, jnp.int32)
        _ctx_768P = jax.random.normal(jax.random.fold_in(_rk, 11), (16, 16, 192), jnp.float32)
        _ctx_768c = jax.random.dirichlet(jax.random.fold_in(_rk, 511), 0.3 * jnp.ones((16,), jnp.float32), (16, 256))
        _ctx_768t = jnp.einsum('bsk,bkd->bsd', _ctx_768c, _ctx_768P)
        _ctx_768t = _ctx_768t * jax.lax.rsqrt(jnp.mean(jnp.square(_ctx_768t)) + 1e-12) * 0.953939
        ctx_768 = -0.000191848 + 0.999787 * (_ctx_768t + 0.3 * jax.random.normal(jax.random.fold_in(_rk, 611), (16, 256, 192), jnp.float32))
        return (x, ctx_768)
    x, ctx_768 = _rec_inputs()

    def _L0_xattn_setup():
        import jax, jax.numpy as jnp
        import numpy as np
        HEADS = 16
        DIM_HEAD = 64
        QUERY_DIM = 256
        CONTEXT_DIM = 192
        INNER = HEADS * DIM_HEAD
        SCALE = DIM_HEAD ** (-0.5)
        key = jax.random.key(seed)
        ks = jax.random.split(key, 7)
        B, Sq, Skv = (4, 512, 512)
        x = jax.random.normal(ks[0], (B, Sq, QUERY_DIM), dtype=jnp.float32)
        context = jax.random.normal(ks[1], (B, Skv, CONTEXT_DIM), dtype=jnp.float32)
        w_q = jax.random.normal(ks[2], (QUERY_DIM, INNER), dtype=jnp.float32) / np.sqrt(QUERY_DIM)
        w_k = jax.random.normal(ks[3], (CONTEXT_DIM, INNER), dtype=jnp.float32) / np.sqrt(CONTEXT_DIM)
        w_v = jax.random.normal(ks[4], (CONTEXT_DIM, INNER), dtype=jnp.float32) / np.sqrt(CONTEXT_DIM)
        w_o = jax.random.normal(ks[5], (INNER, QUERY_DIM), dtype=jnp.float32) / np.sqrt(INNER)
        b_o = jax.random.normal(ks[6], (QUERY_DIM,), dtype=jnp.float32) * 0.02
        return {'x': x, 'context': context, 'w_q': w_q, 'w_k': w_k, 'w_v': w_v, 'w_o': w_o, 'b_o': b_o}
    _L0_xattn_all = _L0_xattn_setup()
    _L0_xattn_in = {k: v for k, v in _L0_xattn_all.items() if k in ('w_q', 'w_k', 'w_v', 'w_o', 'b_o')}
    del _L0_xattn_all

    def _L0_ffn_setup():
        import math
        import jax, jax.numpy as jnp
        import numpy as np
        D_MODEL = 256
        D_HIDDEN = 1024
        N_EXPERTS = 8
        TOP_K = 2
        CAPACITY_FACTOR = 1.25
        key = jax.random.key(seed)
        ks = jax.random.split(key, 8)
        s = 0.02
        x = jax.random.normal(ks[0], (4, 512, D_MODEL), dtype=jnp.float32)
        router_w = jax.random.normal(ks[1], (D_MODEL, N_EXPERTS), dtype=jnp.float32) * s
        router_b = jnp.zeros((N_EXPERTS,), dtype=jnp.float32)
        w1 = jax.random.normal(ks[2], (N_EXPERTS, D_MODEL, D_HIDDEN), dtype=jnp.float32) * s
        b1 = jnp.zeros((N_EXPERTS, D_HIDDEN), dtype=jnp.float32)
        w2 = jax.random.normal(ks[3], (N_EXPERTS, D_HIDDEN, D_MODEL), dtype=jnp.float32) * s
        b2 = jnp.zeros((N_EXPERTS, D_MODEL), dtype=jnp.float32)
        return {'x': x, 'router_w': router_w, 'router_b': router_b, 'w1': w1, 'b1': b1, 'w2': w2, 'b2': b2}
    _L0_ffn_all = _L0_ffn_setup()
    _L0_ffn_in = {k: v for k, v in _L0_ffn_all.items() if k in ('router_w', 'router_b', 'w1', 'b1', 'w2', 'b2')}
    del _L0_ffn_all
    return {'x': x, 'ctx_768': ctx_768, 'L0_xattn_w_q': _L0_xattn_in['w_q'], 'L0_xattn_w_k': _L0_xattn_in['w_k'], 'L0_xattn_w_v': _L0_xattn_in['w_v'], 'L0_xattn_w_o': _L0_xattn_in['w_o'], 'L0_xattn_b_o': _L0_xattn_in['b_o'], 'L0_ffn_router_w': _L0_ffn_in['router_w'], 'L0_ffn_router_b': _L0_ffn_in['router_b'], 'L0_ffn_w1': _L0_ffn_in['w1'], 'L0_ffn_b1': _L0_ffn_in['b1'], 'L0_ffn_w2': _L0_ffn_in['w2'], 'L0_ffn_b2': _L0_ffn_in['b2']}

def reference(x, ctx_768, L0_xattn_w_q, L0_xattn_w_k, L0_xattn_w_v, L0_xattn_w_o, L0_xattn_b_o, L0_ffn_router_w, L0_ffn_router_b, L0_ffn_w1, L0_ffn_b1, L0_ffn_w2, L0_ffn_b2):
    import jax
    import jax.numpy as jnp

    def _L0_xattn_ref(x, context, w_q, w_k, w_v, w_o, b_o):
        import jax, jax.numpy as jnp
        import numpy as np
        HEADS = 16
        DIM_HEAD = 64
        QUERY_DIM = 256
        CONTEXT_DIM = 192
        INNER = HEADS * DIM_HEAD
        SCALE = DIM_HEAD ** (-0.5)
        B, Sq, _ = x.shape
        Skv = context.shape[1]
        q = (x @ w_q).reshape(B, Sq, HEADS, DIM_HEAD).transpose(0, 2, 1, 3)
        k = (context @ w_k).reshape(B, Skv, HEADS, DIM_HEAD).transpose(0, 2, 1, 3)
        v = (context @ w_v).reshape(B, Skv, HEADS, DIM_HEAD).transpose(0, 2, 1, 3)
        sim = jnp.einsum('bhid,bhjd->bhij', q, k) * SCALE
        attn = jax.nn.softmax(sim, axis=-1)
        out = jnp.einsum('bhij,bhjd->bhid', attn, v)
        out = out.transpose(0, 2, 1, 3).reshape(B, Sq, INNER)
        return out @ w_o + b_o

    def _L0_ffn_ref(x, router_w, router_b, w1, b1, w2, b2):
        import math
        import jax, jax.numpy as jnp
        import numpy as np
        D_MODEL = 256
        D_HIDDEN = 1024
        N_EXPERTS = 8
        TOP_K = 2
        CAPACITY_FACTOR = 1.25
        B, T, D = x.shape
        N = B * T
        E = N_EXPERTS
        capacity = max(1, math.ceil(N / E * CAPACITY_FACTOR))
        x_flat = x.reshape(N, D)
        logits = x_flat.astype(jnp.float32) @ router_w + router_b
        gates = jax.nn.softmax(logits, axis=-1)
        _, topk_idx = jax.lax.top_k(gates, TOP_K)
        expert_mask = jax.nn.one_hot(topk_idx, E, dtype=jnp.int32).sum(1)
        pos = jnp.cumsum(expert_mask, axis=0) - 1
        expert_mask = expert_mask * (pos < capacity)
        valid = expert_mask > 0
        pos_c = jnp.where(valid, pos, capacity)
        e_idx = jnp.broadcast_to(jnp.arange(E), (N, E))
        dispatched = x_flat[:, None, :] * valid[:, :, None].astype(x.dtype)
        buf = jnp.zeros((E, capacity + 1, D), x.dtype).at[e_idx.ravel(), pos_c.ravel()].add(dispatched.reshape(N * E, D))
        buf = buf[:, :capacity]
        h = jax.nn.gelu(jnp.einsum('ecd,edh->ech', buf, w1) + b1[:, None, :], approximate=False)
        out = jnp.einsum('ech,ehd->ecd', h, w2) + b2[:, None, :]
        pos_g = jnp.minimum(pos_c, capacity - 1)
        gathered = out[e_idx, pos_g]
        weights = (gates * valid).astype(x.dtype)
        y = jnp.einsum('ned,ne->nd', gathered, weights)
        return y.reshape(B, T, D)
    x = x + _L0_xattn_ref(_layernorm(x, axis=-1), ctx_768, L0_xattn_w_q, L0_xattn_w_k, L0_xattn_w_v, L0_xattn_w_o, L0_xattn_b_o)
    x = x + _L0_ffn_ref(_layernorm(x, axis=-1), L0_ffn_router_w, L0_ffn_router_b, L0_ffn_w1, L0_ffn_b1, L0_ffn_w2, L0_ffn_b2)
    return x

_drawn_inputs = setup_inputs


def setup_inputs(seed=0):
    import zlib

    import numpy as np

    out = dict(_drawn_inputs(seed))
    spreads = {'L0_ffn_router_b': (0.0, 0.522), 'L0_ffn_b1': (0.0, 0.8), 'L0_ffn_b2': (0.0, 0.451)}
    factors = {'L0_xattn_b_o': 3.004, 'L0_ffn_w1': 2.932, 'L0_ffn_w2': 2.731}
    for name, (base, spread) in spreads.items():
        noise = np.random.default_rng([zlib.crc32(name.encode()), seed]).standard_normal(out[name].shape)
        drawn = base * np.exp(spread * noise) if base else spread * noise
        out[name] = jnp.asarray(drawn.astype(out[name].dtype))
    for name, factor in factors.items():
        out[name] = (out[name] * factor).astype(out[name].dtype)
    return out
```

```python
from contextlib import ExitStack

import concourse.bass as bass
from concourse import mybir

F32 = mybir.dt.float32
F32R = mybir.dt.float32r
BF16 = mybir.dt.bfloat16
I32 = mybir.dt.int32
ALU = mybir.AluOpType
ACT = mybir.ActivationFunctionType
AX = mybir.AxisListType

P = 128
B, S, D = 16, 256, 256
CD = 192
HD = 64
INNER = 1024
PAIRS = INNER // P
ST = S // P
DC = D // P
NE, HID = 8, 1024
HC = HID // P
N = B * S
CAP = -(-N * 5 // (NE * 4))
ET = CAP // P
EPS = 1e-5
SCALE = HD ** -0.5
BIG = 65536.0
ID, GATE = D, D + 1
ROW = D + 1 + NE
HALF = CAP // 2
STEPS = B * PAIRS
assert CAP == ET * P and CAP % 2 == 0 and HALF <= 512


def timeline():
    out = [("split", w) for w in range(3)]
    out += [("ln1_stats", 0), ("ctx", 0), ("ln1", 0), ("xt", 0), ("q", 0), ("k", 0)]
    out += [("v", n) for n in range(4)]
    out += [("split", 3), ("ln1_stats", 1), ("ctx", 1), ("ln1", 1)]
    for i in range(STEPS + PAIRS + 1):
        b, c = divmod(i, PAIRS)
        live = i < STEPS
        item = i // 2 + 1
        if live:
            out += [("scores", i)]
        if 1 <= i <= STEPS:
            out += [("norm0", i - 1)]
        if 1 <= i <= STEPS:
            out += [("norm1", i - 1)]
        if item < STEPS // 2:
            out += [("q" if i % 2 == 0 else "k", item)]
        if live:
            out += [("exp1", i)]
        if 2 <= i < STEPS + 2:
            out += [("pv", i - 2)]
        if b + 1 < B:
            out += {0: [("xt", b + 1)], 4: [("v", 4 * b + 4)], 5: [("v", 4 * b + 5)],
                    6: [("v", 4 * b + 6)], 7: [("v", 4 * b + 7)]}.get(c, [])
        if 0 <= b - 1 < B:
            out += {2: [("o", ST * (b - 1))], 3: [("o", ST * (b - 1) + 1), ("ln2_stats", b - 1)],
                    4: [("ln2", b - 1)], 5: [("x2t", b - 1)], 6: [("logits", b - 1)],
                    7: [("gate", b - 1)]}.get(c, [])
        if c == 0 and b >= 2:
            out += [("pos", b - 2), ("slot", b - 2)]
        if b + 2 < B:
            out += {5: [("ln1_stats", b + 2)], 6: [("ln1", b + 2), ("ctx", b + 2)]}.get(c, [])
        if 1 <= i <= STEPS:
            out += [("turn", i - 1)]
    return out


TIMELINE = timeline()
WORKS = [(s, n) for s, n in TIMELINE if s in ("xt", "q", "k", "v", "o", "x2t", "logits", "pos")]
WORK_READ = {"xt": "xt_lo", "q": "q_lo", "k": "k_lo", "v": "v_sb", "o": "x2", "x2t": "x2t_sb",
             "logits": "biased", "pos": "slots"}


def build(nc, x, ctxt, wq, wk, wv, wo, bo, rw, rb, w1, b1, w2, b2, out):
    es = ExitStack()
    with es:
        sems = {}

        def sem(name):
            if name not in sems:
                sems[name] = es.enter_context(nc.semaphore("s_" + name))
            return sems[name]

        def sb(stack, name, shape, dt=F32):
            return stack.enter_context(nc.sbuf_tensor(name, [P, *shape], dt))

        psum = es.enter_context(nc.psum_tensor("psum", [P, 8, 512], F32))
        table = nc.dram_tensor("slot_table", [NE * CAP, ROW], F32, kind="Internal").ap()

        ident = sb(es, "ident", [P])
        b1t = sb(es, "b1t", [NE, HC])
        first = ExitStack()
        wqh, wql = (sb(first, n, [DC, INNER], F32R) for n in ("wqh", "wql"))
        wkh, wkl = (sb(first, n, [2, INNER], F32R) for n in ("wkh", "wkl"))
        wvh, wvl = (sb(first, n, [2, INNER], F32R) for n in ("wvh", "wvl"))
        rest = ExitStack()
        woh, wol = (sb(rest, n, [PAIRS, D], F32R) for n in ("woh", "wol"))
        xin = sb(rest, "xin", [3, ST, D])
        xn = sb(rest, "xn", [ST, D])
        xth, xtl = (sb(rest, n, [2, DC, S], F32R) for n in ("xth", "xtl"))
        c0 = sb(rest, "c0", [2, S])
        c1 = sb(rest, "c1", [2, S])
        c0h, c0l = (sb(rest, n, [2, S], F32R) for n in ("c0h", "c0l"))
        c1s = sb(rest, "c1s", [2, S], F32R)
        c1t = sb(rest, "c1t", [S], F32R)
        qh, ql = (sb(rest, n, [2, 2, S], F32R) for n in ("qh", "ql"))
        kh, kl = (sb(rest, n, [2, 2, 2, S], F32R) for n in ("kh", "kl"))
        v = sb(rest, "v", [2, ST, INNER])
        prob = sb(rest, "prob", [2, 2, 2, S])
        probt = sb(rest, "probt", [2, 2, ST, S])
        ah, al = (sb(rest, n, [2, PAIRS, S], F32R) for n in ("ah", "al"))
        x2 = sb(rest, "x2", [2, ST, D])
        row = sb(rest, "row", [2, ST, ROW])
        x2t = sb(rest, "x2t", [DC, S])
        blank = sb(rest, "blank", [ET, ROW])
        bo_all = sb(rest, "bo_all", [D])
        rwt = sb(rest, "rwt", [DC, NE])
        rb_all = sb(rest, "rb_all", [NE])
        upto = sb(rest, "upto", [P], BF16)
        ones = sb(rest, "ones", [P], BF16)
        lower = sb(rest, "lower", [NE, NE])
        slot0i = sb(rest, "slot0i", [NE], I32)
        slot0 = sb(rest, "slot0", [NE])
        toki = sb(rest, "toki", [ST], I32)
        tok = sb(rest, "tok", [ST])
        dumpi = sb(rest, "dumpi", [ET], I32)
        negmax = sb(rest, "negmax", [2, 2, 2])
        total = sb(rest, "total", [2, 2, 2])
        invtot = sb(rest, "invtot", [2, 2, 2])
        stats = sb(rest, "stats", [ST, 6])
        mean_var = {n: sb(rest, n + "_mean_var", [ST, 2]) for n in ("ln1", "ln2")}
        rstd = {n: sb(rest, n + "_rstd", [ST]) for n in ("ln1", "ln2")}
        shifted, newton, power = (sb(rest, n, [ST]) for n in ("shifted", "newton", "power"))
        logit, lexp, gates = (sb(rest, n, [ST, NE]) for n in ("logit", "lexp", "gates"))
        lmax, lsum, linv = (sb(rest, n, [ST]) for n in ("lmax", "lsum", "linv"))
        above, equal = (sb(rest, n, [ST, NE, NE]) for n in ("above", "equal"))
        rank, slot, valid, lowkey, highkey = (sb(rest, n, [ST, NE])
                                              for n in ("rank", "slot", "valid", "lowkey", "highkey"))
        chosen = sb(rest, "chosen", [ST, NE], BF16)
        before = sb(rest, "before", [NE], BF16)
        pick, same = (sb(rest, n, [2, ST]) for n in ("pick", "same"))
        picki = sb(rest, "picki", [2, 2, ST], I32)
        rest.close()
        first.close()
        late = es.enter_context(ExitStack())
        w1r, w2r = sb(late, "w1r", [DC, HID]), sb(late, "w2r", [HC, D])
        w1h, w1l, w2h, w2l = [], [], [], []
        for r in range(2):
            w1h.append(sb(late, f"w1h{r}", [DC, HID], F32R))
            w1l.append(sb(late, f"w1l{r}", [DC, HID], F32R))
            w2h.append(sb(late, f"w2h{r}", [HC, D], F32R))
            w2l.append(sb(late, f"w2l{r}", [HC, D], F32R))
        hidh, hidl = (sb(late, n, [HC, CAP], F32R) for n in ("hidh", "hidl"))
        hid = sb(late, "hid", [2, CAP])
        bufh, bufl = (sb(late, n, [2, DC, CAP], F32R) for n in ("bufh", "bufl"))
        rows = sb(late, "rows", [2, ET, ROW])
        rowi = sb(late, "rowi", [2, ET], I32)
        y = sb(late, "y", [2, ET, D])
        b2_all = sb(late, "b2_all", [NE, D])

        out_rows = out
        block = es.enter_context(nc.Block())

        def all_stored(eng):
            eng.wait_ge(sem("spare_clear"), 16)
            for r in range(2):
                eng.wait_ge(sem(f"x2_out{r}"), 16 * B // 2)

        ring3 = lambda n: n % 3

        @block.sync
        def _(sp):
            def load_x(b):
                if b >= 3:
                    sp.wait_ge(sem("x2"), ST * (b - 2))
                sp.dma_start(xin[:, ring3(b), :, :], x[b].rearrange("(t p) d -> p t d", p=P))\
                  .then_inc(sem(f"x_in{ring3(b)}"), 16)

            def load_ctx(b):
                if b >= 2:
                    sp.wait_ge(sem("ctx"), b - 1)
                cols = slice(b * S, (b + 1) * S)
                sp.dma_start(c0[:, b % 2, :], ctxt[0:P, cols]).then_inc(sem(f"ctx_in{b % 2}"), 16)
                for h in range(2):
                    sp.dma_start(c1[h * HD:(h + 1) * HD, b % 2, :], ctxt[P:CD, cols])\
                      .then_inc(sem(f"ctx_in{b % 2}"), 16)

            sp.dma_start(v[:, 0, :, :], wq.rearrange("(k p) n -> p k n", p=P)).then_inc(sem("w_in0"), 16)
            load_x(0)
            load_ctx(0)
            for which, w, dst in ((1, wk, v[:, 1, :, :]), (2, wv, probt[:, :, :, :, :]
                                  .rearrange("p a b c d -> p (a b c d)").rearrange("p (k n) -> p k n", k=2))):
                sp.dma_start(dst[:, 0, :], w[0:P, :]).then_inc(sem(f"w_in{which}"), 16)
                for h in range(2):
                    sp.dma_start(dst[h * HD:(h + 1) * HD, 1, :], w[P:CD, :])\
                      .then_inc(sem(f"w_in{which}"), 16)
            sp.dma_start(prob[:, :, :, :, :].rearrange("p a b c d -> p (a b c d)")
                         .rearrange("p (k n) -> p k n", k=PAIRS),
                         wo.rearrange("(k p) n -> p k n", p=P)).then_inc(sem("w_in3"), 16)
            for b in (1, 2):
                load_x(b)
            load_ctx(1)
            sp.dma_start(bo_all[:, :], bo.partition_broadcast(P)).then_inc(sem("const_in"), 16)
            sp.dma_start(rb_all[:, :], rb.partition_broadcast(P)).then_inc(sem("const_in"), 16)
            sp.dma_start(rwt[:, :, :], rw.rearrange("(k p) n -> p k n", p=P)).then_inc(sem("const_in"), 16)
            sp.dma_start(b1t[:, :, :], b1).then_inc(sem("b1_in"), 16)
            sp.wait_ge(sem("blank"), 1)
            for e in range(NE):
                sp.dma_start(table[e * CAP:(e + 1) * CAP, :].rearrange("(s p) w -> p s w", p=P),
                             blank[:, :, :]).then_inc(sem("table_clear"), 16)
            sp.dma_start(out_rows[N:N + CAP, :].rearrange("(s p) w -> p s w", p=P),
                         blank[:, :, 0:D]).then_inc(sem("spare_clear"), 16)
            for b in range(B):
                if b + 2 < B:
                    load_ctx(b + 2)
                if b + 3 < B:
                    load_x(b + 3)
                sp.wait_ge(sem("x2"), ST * (b + 1))
                sp.dma_start(out_rows[b * S:(b + 1) * S, :].rearrange("(t p) d -> p t d", p=P),
                             x2[:, b % 2, :, :]).then_inc(sem(f"x2_out{b % 2}"), 16)

            sp.wait_ge(sem("q"), STEPS // 2)
            sp.wait_ge(sem("k"), STEPS // 2)
            sp.wait_ge(sem("v"), 4 * B)

            def load_w(e):
                if e >= 1:
                    sp.wait_ge(sem("wsplit_hi"), 2 * e)
                    sp.wait_ge(sem("wsplit_lo"), 2 * e)
                sp.dma_start(w1r[:, :, :], w1[e].rearrange("(k p) n -> p k n", p=P)).then_inc(sem("w1_in"), 16)
                sp.dma_start(w2r[:, :, :], w2[e].rearrange("(k p) n -> p k n", p=P)).then_inc(sem("w2_in"), 16)

            def load_rows(e):
                if e >= 2:
                    sp.wait_ge(sem("y"), ET * (e - 1))
                sp.dma_start(rows[:, e % 2, :, :],
                             table[e * CAP:(e + 1) * CAP, :].rearrange("(s p) w -> p s w", p=P))\
                  .then_inc(sem(f"rows_in{e % 2}"), 16)

            load_w(0)
            sp.wait_ge(sem("scatter"), 16 * 2 * ST * B)
            all_stored(sp)
            load_rows(0)
            sp.dma_start(b2_all[:, :, :], b2.partition_broadcast(P)).then_inc(sem("b2_in"), 16)
            load_rows(1)
            for e in range(1, NE):
                load_w(e)
                if e + 1 < NE:
                    load_rows(e + 1)
            sp.wait_ge(sem("added"), 16 * ET * NE)

        @block.gpsimd
        def _(pool):
            done = [0]

            def link(ins):
                done[0] += 1
                ins.then_inc(sem("pool"), 1)
                pool.wait_ge(sem("pool"), done[0])

            def link_as(name, ins):
                ins.then_inc(sem(name), 1)
                told[name] = told.get(name, 0) + 1
                pool.wait_ge(sem(name), told[name])

            told = {}

            link(pool.memset(power[:, :], -0.5))
            link(pool.memset(ident[:, :], 0.0))
            link_as("ident", pool.affine_select(out=ident[:, :], in_=ident[:, :], compare_op=ALU.not_equal,
                                                fill=1.0, base=0, pattern=[[-1, P]], channel_multiplier=1))
            for t in (kh, kl):
                link_as("kzero", pool.memset(t[HD:P, :, :, 0, :].bitcast(F32), 0.0))
                link_as("kzero", pool.memset(t[0:HD, :, :, 1, :].bitcast(F32), 0.0))

            def ctx(b):
                p = b % 2
                pool.wait_ge(sem(f"ctx_in{p}"), 48 * (b // 2 + 1))
                if b >= 2:
                    pool.wait_ge(sem("k"), 4 * (b - 1))
                    pool.wait_ge(sem("v"), 4 * (b - 1))
                link(pool.tensor_copy(c1s[0:HD, p, :], c1[0:HD, p, :]))
                link(pool.tensor_copy(c1t[HD:P, :], c1[HD:P, p, :]))
                link(pool.tensor_copy(c0h[:, p, :], c0[:, p, :]))
                link(pool.tensor_tensor(c1s[HD:P, p, :], c1[HD:P, p, :], c1t[HD:P, :].bitcast(F32), ALU.subtract))
                link_as("ctx", pool.tensor_tensor(c0l[:, p, :], c0[:, p, :], c0h[:, p, :].bitcast(F32),
                                                  ALU.subtract))

            def inverse_root(which, n):
                pool.wait_ge(sem(f"{which}_var"), n + 1)
                if n >= 1:
                    pool.wait_ge(sem(which), n)
                root = rstd[which][:, :]
                link(pool.tensor_scalar(shifted[:, :], mean_var[which][:, :, 1], EPS, None, ALU.add))
                link(pool.tensor_tensor(root, shifted[:, :], power[:, :], ALU.pow))
                link(pool.tensor_tensor(newton[:, :], root, root, ALU.mult))
                link(pool.tensor_tensor(newton[:, :], newton[:, :], shifted[:, :], ALU.mult))
                link(pool.tensor_scalar(newton[:, :], newton[:, :], -0.5, 1.5, ALU.mult, ALU.add))
                link_as(f"{which}_rstd", pool.tensor_tensor(root, root, newton[:, :], ALU.mult))

            def ln1(b):
                pool.wait_ge(sem("const_in"), 48)
                pool.wait_ge(sem("ln1"), b + 1)
                for t in range(ST):
                    link_as("residual", pool.tensor_tensor(xin[:, ring3(b), t, :], xin[:, ring3(b), t, :],
                                                           bo_all[:, :], ALU.add))

            def constants():
                link(pool.memset(upto[:, :], 1.0))
                link(pool.affine_select(out=upto[:, :], in_=upto[:, :], compare_op=ALU.is_ge, fill=0.0, base=0,
                                        pattern=[[1, P]], channel_multiplier=-1))
                link(pool.memset(ones[:, :], 1.0))
                link(pool.memset(before[:, :], 0.0))
                link(pool.memset(lower[:, :, :], 1.0))
                link(pool.affine_select(out=lower[:, :, :], in_=lower[:, :, :], compare_op=ALU.is_gt, fill=0.0,
                                        base=0, pattern=[[1, NE], [-1, NE]], channel_multiplier=0))
                link(pool.iota(slot0i[:, :], pattern=[[CAP, NE]], base=-1, channel_multiplier=0))
                link(pool.iota(dumpi[:, :], pattern=[[P, ET]], base=N, channel_multiplier=1))
                link(pool.iota(toki[:, :], pattern=[[P, ST]], base=0, channel_multiplier=1))
                link(pool.tensor_copy(slot0[:, :], slot0i[:, :]))
                link(pool.tensor_copy(tok[:, :], toki[:, :]))
                link(pool.memset(blank[:, :, :], 0.0))
                link_as("blank", pool.tensor_copy(blank[:, :, ID], dumpi[:, :]))

            def slots(b):
                if b == 0:
                    pool.wait_ge(sem("table_clear"), 16 * NE)
                pool.wait_ge(sem("picks"), b + 1)
                for k in range(2):
                    for t in range(ST):
                        pool.indirect_dma_start(
                            out=table, out_offset=bass.IndirectOffsetOnAxis(ap=picki[:, b % 2, k, t:t + 1], axis=0),
                            in_=row[:, b % 2, t, :], in_offset=None, bounds_check=NE * CAP - 1,
                            oob_is_err=False).then_inc(sem("scatter"), 16)
                pool.wait_ge(sem("scatter"), 16 * 2 * ST * (b + 1))

            did = set()
            for stage, n in TIMELINE:
                if stage == "ctx":
                    ctx(n)
                if stage in ("ln1_stats", "ln2_stats"):
                    inverse_root(stage[:3], n)
                if stage == "ln1":
                    if n == 1 and "c" not in did:
                        did.add("c")
                        constants()
                    ln1(n)
                if stage == "slot":
                    slots(n)

            all_stored(pool)
            for e in range(NE):
                pool.wait_ge(sem("rowi"), e + 1)
                if e >= 1:
                    pool.wait_ge(sem("added"), 16 * ET * e)
                for s in range(ET):
                    pool.wait_ge(sem("y"), ET * e + s + 1)
                    pool.indirect_dma_start(
                        out=out_rows, out_offset=bass.IndirectOffsetOnAxis(ap=rowi[:, e % 2, s:s + 1], axis=0),
                        in_=y[:, e % 2, s, :], in_offset=None, bounds_check=N + CAP - 1, oob_is_err=True,
                        compute_op=ALU.add).then_inc(sem("added"), 16)

        @block.tensor
        def _(pe):
            work = {w: n for n, w in enumerate(WORKS)}

            def bank(stage, n):
                at = work[stage, n]
                if at >= 2:
                    s, m = WORKS[at - 2]
                    pe.wait_ge(sem(WORK_READ[s]), m + 1)
                return psum[:, 6 + at % 2, :]

            def products(dst, terms):
                for j, (lhs, rhs) in enumerate(terms):
                    mm = pe.matmul(dst, lhs, rhs, start=(j == 0), stop=(j == len(terms) - 1))
                return mm

            def xt(b):
                dst = bank("xt", b)
                pe.wait_ge(sem("ln1"), b + 1)
                for k in range(DC):
                    for t in range(ST):
                        mm = pe.transpose(dst[:, k * S + t * P:k * S + (t + 1) * P],
                                          xn[:, t, k * P:(k + 1) * P], ident[:, :])
                mm.then_inc(sem("xt"), 1)

            def q(n):
                b, dst = n // 4, bank("q", n)
                pe.wait_ge(sem("xt_lo"), b + 1)
                if n == 0:
                    pe.wait_ge(sem("split_lo"), 1)
                for cc in range(2):
                    cols = slice((n % 4 * 2 + cc) * P, (n % 4 * 2 + cc + 1) * P)
                    mm = products(dst[:, cc * S:(cc + 1) * S],
                                  [(w[:, k, cols], a[:, b % 2, k, :]) for k in range(DC)
                                   for w, a in ((wqh, xth), (wqh, xtl), (wql, xth))])
                mm.then_inc(sem("q"), 1)

            def k(n):
                b, dst = n // 4, bank("k", n)
                pe.wait_ge(sem("ctx"), b + 1)
                if n == 0:
                    pe.wait_ge(sem("split_lo"), 2)
                for cc in range(2):
                    cols = slice((n % 4 * 2 + cc) * P, (n % 4 * 2 + cc + 1) * P)
                    mm = products(dst[:, cc * S:(cc + 1) * S],
                                  [(wkh[:, 0, cols], c0h[:, b % 2, :]), (wkh[:, 0, cols], c0l[:, b % 2, :]),
                                   (wkl[:, 0, cols], c0h[:, b % 2, :]), (wkh[:, 1, cols], c1s[:, b % 2, :]),
                                   (wkl[:, 1, cols], c1s[:, b % 2, :])])
                mm.then_inc(sem("k"), 1)

            def v_(n):
                b, half, t = n // 4, n % 4 // 2, n % 2
                dst = bank("v", n)
                pe.wait_ge(sem("ctx"), b + 1)
                if n == 0:
                    pe.wait_ge(sem("split_lo"), 3)
                cols, tt = slice(half * 512, half * 512 + 512), slice(t * P, (t + 1) * P)
                products(dst, [(c0h[:, b % 2, tt], wvh[:, 0, cols]), (c0l[:, b % 2, tt], wvh[:, 0, cols]),
                               (c0h[:, b % 2, tt], wvl[:, 0, cols]), (c1s[:, b % 2, tt], wvh[:, 1, cols]),
                               (c1s[:, b % 2, tt], wvl[:, 1, cols])]).then_inc(sem("v"), 1)

            def scores(i):
                n, cc = i // 2, i % 2
                pe.wait_ge(sem("q_lo"), n + 1)
                pe.wait_ge(sem("k_lo"), n + 1)
                for qb in range(ST):
                    if i >= 1:
                        pe.wait_ge(sem("exp"), 2 * (i - 1) + qb + 1)
                    cols = slice(qb * P, (qb + 1) * P)
                    both = lambda t: t[:, n % 2, cc, :, :].rearrange("p h s -> p (h s)")
                    products(psum[:, qb, :],
                             [(qh[:, n % 2, cc, cols], both(kh)), (qh[:, n % 2, cc, cols], both(kl)),
                              (ql[:, n % 2, cc, cols], both(kh))]).then_inc(sem("scores"), 1)

            def turn(i):
                for h in range(2):
                    if i >= 1:
                        pe.wait_ge(sem("probt"), 2 * (i - 1) + h + 1)
                    for qb in range(ST):
                        pe.wait_ge(sem("norm"), 2 * i + qb + 1)
                        for kb in range(ST):
                            mm = pe.transpose(psum[:, 2 + h, kb * S + qb * P:kb * S + (qb + 1) * P],
                                              prob[:, i % 2, qb, h, kb * P:(kb + 1) * P], ident[:, :])
                    mm.then_inc(sem("turn"), 1)

            def pv(i):
                b, c = divmod(i, PAIRS)
                pe.wait_ge(sem("v_sb"), 4 * (b + 1))
                if i >= 2:
                    pe.wait_ge(sem("a_lo"), i - 1)
                pe.wait_ge(sem("probt"), 2 * (i + 1))
                for h in range(2):
                    for kb in range(ST):
                        cols = slice((2 * c + h) * HD, (2 * c + h + 1) * HD)
                        mm = pe.matmul(psum[h * HD:(h + 1) * HD, 4 + i % 2, 0:S], v[:, b % 2, kb, cols],
                                       probt[:, i % 2, h, kb, :], start=(kb == 0), stop=(kb == ST - 1))
                mm.then_inc(sem("pv"), 1)

            def o(n):
                b, t = divmod(n, ST)
                dst, tt = bank("o", n), slice(t * P, (t + 1) * P)
                pe.wait_ge(sem("a_lo"), PAIRS * (b + 1))
                if n == 0:
                    pe.wait_ge(sem("split_lo"), 4)
                products(dst[:, 0:D], [(a[:, b % 2, c, tt], w[:, c, :]) for c in range(PAIRS)
                                       for a, w in ((ah, woh), (ah, wol), (al, woh))]).then_inc(sem("o"), 1)

            def x2t_(b):
                dst = bank("x2t", b)
                pe.wait_ge(sem("ln2"), b + 1)
                for k in range(DC):
                    for t in range(ST):
                        mm = pe.transpose(dst[:, k * S + t * P:k * S + (t + 1) * P],
                                          row[:, b % 2, t, k * P:(k + 1) * P], ident[:, :])
                mm.then_inc(sem("x2t"), 1)

            def logits(b):
                dst = bank("logits", b)
                pe.wait_ge(sem("x2t_sb"), b + 1)
                for t in range(ST):
                    mm = products(dst[:, t * NE:(t + 1) * NE],
                                  [(x2t[:, k, t * P:(t + 1) * P], rwt[:, k, :]) for k in range(DC)])
                mm.then_inc(sem("logits"), 1)

            def pos(b):
                dst = bank("pos", b)
                pe.wait_ge(sem("chosen"), b + 1)
                products(dst[:, 0:NE], [(upto[:, :], chosen[:, 0, :]), (ones[:, :], before[:, :])])
                products(dst[:, NE:2 * NE], [(upto[:, :], chosen[:, 1, :]), (ones[:, :], chosen[:, 0, :]),
                                             (ones[:, :], before[:, :])]).then_inc(sem("pos"), 1)

            pe.wait_ge(sem("ident"), 1)
            steps = dict(xt=xt, q=q, k=k, v=v_, scores=scores, turn=turn, pv=pv, o=o, x2t=x2t_, logits=logits, pos=pos)
            for stage, n in TIMELINE:
                if stage in steps:
                    steps[stage](n)

            units = [(e, u) for e in range(NE) for u in range(3)]

            def turn_rows(e):
                pe.wait_ge(sem(f"rows_in{e % 2}"), 16 * (e // 2 + 1))
                for u in range(3):
                    at = 3 * e + u
                    if at >= 2:
                        pe.wait_ge(sem("buf_lo"), at - 1)
                    for s in range(2 * u, min(2 * u + 2, ET)):
                        for kk in range(DC):
                            col = (s - 2 * u) * D + kk * P
                            mm = pe.transpose(psum[:, 6 + at % 2, col:col + P],
                                              rows[:, e % 2, s, kk * P:(kk + 1) * P], ident[:, :])
                    mm.then_inc(sem("turn_rows"), 1)

            def up(e):
                r = e % 2
                pe.wait_ge(sem("buf_lo"), 3 * (e + 1))
                pe.wait_ge(sem("wsplit_hi"), 2 * e + 1)
                pe.wait_ge(sem("wsplit_lo"), 2 * e + 1)
                for j in range(HC):
                    at = HC * e + j
                    if at >= 2:
                        pe.wait_ge(sem("gelu"), at - 1)
                    cols = slice(j * P, (j + 1) * P)
                    for half in range(2):
                        hs = slice(half * HALF, (half + 1) * HALF)
                        mm = products(psum[:, 2 * (at % 2) + half, 0:HALF],
                                      [(w[:, kk, cols], a[:, r, kk, hs]) for kk in range(DC)
                                       for w, a in ((w1h[r], bufh), (w1h[r], bufl), (w1l[r], bufh))])
                    mm.then_inc(sem("up"), 1)

            def down(e):
                r = e % 2
                pe.wait_ge(sem("wsplit_hi"), 2 * e + 2)
                pe.wait_ge(sem("wsplit_lo"), 2 * e + 2)
                for s in range(ET):
                    at = ET * e + s
                    if at >= 2:
                        pe.wait_ge(sem("y"), at - 1)
                    ss = slice(s * P, (s + 1) * P)
                    dst = psum[:, 4 + at % 2, 0:D]
                    for j in range(HC):
                        if s == 0:
                            pe.wait_ge(sem("hid_lo"), HC * e + j + 1)
                        for m, (a, w) in enumerate(((hidh, w2h[r]), (hidh, w2l[r]), (hidl, w2h[r]))):
                            mm = pe.matmul(dst, a[:, j, ss], w[:, j, :], start=(j == 0 and m == 0),
                                           stop=(j == HC - 1 and m == 2))
                    mm.then_inc(sem("down"), 1)

            pe.wait_ge(sem("slots"), B)
            turn_rows(0)
            for e in range(NE):
                up(e)
                if e + 1 < NE:
                    turn_rows(e + 1)
                down(e)

        @block.scalar
        def _(act):
            copy = lambda dst, src, **kw: act.activation(dst, src, ACT.Copy, **kw)
            raw = [v[:, 0, :, :], v[:, 1, :, :],
                   probt[:, :, :, :, :].rearrange("p a b c d -> p (a b c d)").rearrange("p (k n) -> p k n", k=2),
                   prob[:, :, :, :, :].rearrange("p a b c d -> p (a b c d)").rearrange("p (k n) -> p k n", k=PAIRS)]

            def work_bank(stage, n):
                return psum[:, 6 + WORKS.index((stage, n)) % 2, :]

            def split(w):
                act.wait_ge(sem(f"w_in{w}"), 48 if w in (1, 2) else 16)
                copy((wqh, wkh, wvh, woh)[w][:, :, :], raw[w]).then_inc(sem("split_hi"), 1)

            def xt(b):
                act.wait_ge(sem("xt"), b + 1)
                if b >= 2:
                    act.wait_ge(sem("q"), 4 * (b - 1))
                copy(xth[:, b % 2, :, :], work_bank("xt", b).rearrange("p (k s) -> p k s", k=DC))\
                    .then_inc(sem("xt_hi"), 1)

            def q(n):
                act.wait_ge(sem("q"), n + 1)
                if n >= 2:
                    act.wait_ge(sem("scores"), 4 * (n - 1))
                copy(qh[:, n % 2, :, :], work_bank("q", n).rearrange("p (c s) -> p c s", c=2), scale=SCALE)\
                    .then_inc(sem("q_hi"), 1)

            def k(n):
                act.wait_ge(sem("k"), n + 1)
                if n >= 2:
                    act.wait_ge(sem("scores"), 4 * (n - 1))
                if n == 0:
                    act.wait_ge(sem("kzero"), 4)
                src = work_bank("k", n).rearrange("p (c s) -> p c s", c=2)
                for h in range(2):
                    rows_ = slice(h * HD, (h + 1) * HD)
                    last = copy(kh[rows_, n % 2, :, h, :], src[rows_, :, :])
                last.then_inc(sem("k_hi"), 1)

            def v_(n):
                b, half, t = n // 4, n % 4 // 2, n % 2
                act.wait_ge(sem("v"), n + 1)
                if n == 0:
                    act.wait_ge(sem("split_lo"), 2)
                if b >= 2:
                    act.wait_ge(sem("pv"), PAIRS * (b - 1))
                copy(v[:, b % 2, t, half * 512:half * 512 + 512], work_bank("v", n)).then_inc(sem("v_sb"), 1)

            def exps(i, qb):
                act.wait_ge(sem("max"), 2 * i + qb + 1)
                if i == 0:
                    act.wait_ge(sem("split_lo"), 4)
                if i >= 2:
                    act.wait_ge(sem("turn"), 2 * (i - 1))
                for h in range(2):
                    last = act.activation(prob[:, i % 2, qb, h, :], psum[:, qb, h * S:(h + 1) * S], ACT.Exp,
                                          bias=negmax[:, i % 2, qb, h:h + 1],
                                          accum_out=total[:, i % 2, qb, h:h + 1])
                last.then_inc(sem("exp"), 1)

            def turn(i):
                for h in range(2):
                    act.wait_ge(sem("turn"), 2 * i + h + 1)
                    if i >= 2:
                        act.wait_ge(sem("pv"), i - 1)
                    copy(probt[:, i % 2, h, :, :], psum[:, 2 + h, :].rearrange("p (k s) -> p k s", k=ST))\
                        .then_inc(sem("probt"), 1)

            def pv(i):
                b, c = divmod(i, PAIRS)
                act.wait_ge(sem("pv"), i + 1)
                if b >= 2:
                    act.wait_ge(sem("o"), ST * (b - 1))
                copy(ah[:, b % 2, c, :], psum[:, 4 + i % 2, 0:S]).then_inc(sem("a_hi"), 1)

            def x2t_(b):
                act.wait_ge(sem("x2t"), b + 1)
                if b >= 1:
                    act.wait_ge(sem("logits"), b)
                copy(x2t[:, :, :], work_bank("x2t", b).rearrange("p (k s) -> p k s", k=DC))\
                    .then_inc(sem("x2t_sb"), 1)

            def gate(b):
                act.wait_ge(sem("shifted"), b + 1)
                act.activation(lexp[:, :, :], logit[:, :, :], ACT.Exp).then_inc(sem("gate_exp"), 1)

            steps = dict(split=split, xt=xt, q=q, k=k, v=v_, turn=turn, pv=pv, x2t=x2t_, gate=gate,
                         scores=lambda i: exps(i, 0), exp1=lambda i: exps(i, 1))
            for stage, n in TIMELINE:
                if stage in steps:
                    steps[stage](n)

            def split_w(e, part):
                r = e % 2
                act.wait_ge(sem(("w1_in", "w2_in")[part]), 16 * (e + 1))
                if e >= 2:
                    act.wait_ge(sem("down"), ET * (e - 1))
                if e == 1 and part == 0:
                    act.wait_ge(sem("slots"), B)
                    act.wait_ge(sem("scatter"), 16 * 2 * ST * B)
                    all_stored(act)
                copy((w1h, w2h)[part][r][:, :, :], (w1r, w2r)[part][:, :, :]).then_inc(sem("wsplit_hi"), 1)

            def turn_rows(e):
                for u in range(3):
                    at, s0, s1 = 3 * e + u, 2 * u, min(2 * u + 2, ET)
                    act.wait_ge(sem("turn_rows"), at + 1)
                    if e >= 2:
                        act.wait_ge(sem("up"), HC * (e - 1))
                    for kk in range(DC):
                        src = psum[:, 6 + at % 2, :].rearrange("p (s k c) -> p k s c", k=DC, c=P)
                        last = copy(bufh[:, e % 2, kk, s0 * P:s1 * P].rearrange("p (s c) -> p s c", c=P),
                                    src[:, kk, 0:s1 - s0, :])
                    last.then_inc(sem("buf_hi"), 1)

            act.wait_ge(sem("b1_in"), 16)
            act.wait_ge(sem("q"), STEPS // 2)
            act.wait_ge(sem("k"), STEPS // 2)
            act.wait_ge(sem("v"), 4 * B)
            split_w(0, 0)
            split_w(0, 1)
            turn_rows(0)
            for e in range(NE):
                for j in range(HC):
                    at = HC * e + j
                    act.wait_ge(sem("up"), at + 1)
                    if at >= 2:
                        act.wait_ge(sem("hid_lo"), at - 1)
                    act.activation(hid[:, at % 2, :].rearrange("p (a s) -> p a s", a=2),
                                   psum[:, 2 * (at % 2):2 * (at % 2) + 2, 0:HALF], ACT.Gelu,
                                   bias=b1t[:, e, j:j + 1]).then_inc(sem("gelu"), 1)
                    if e + 1 < NE and j in (2, 5):
                        split_w(e + 1, (j - 2) // 3)
                if e + 1 < NE:
                    turn_rows(e + 1)

        @block.vector
        def _(dve):
            done = [0]

            def link(ins):
                done[0] += 1
                ins.then_inc(sem("dve"), 1)
                dve.wait_ge(sem("dve"), done[0])

            raw = [v[:, 0, :, :], v[:, 1, :, :],
                   probt[:, :, :, :, :].rearrange("p a b c d -> p (a b c d)").rearrange("p (k n) -> p k n", k=2),
                   prob[:, :, :, :, :].rearrange("p a b c d -> p (a b c d)").rearrange("p (k n) -> p k n", k=PAIRS)]

            def work_bank(stage, n):
                return psum[:, 6 + WORKS.index((stage, n)) % 2, :]

            def rest_of(dst, whole, head):
                return dve.tensor_tensor(dst, whole, head.bitcast(F32), ALU.subtract)

            def ln_stats(which, n, src):
                if n >= 1:
                    dve.wait_ge(sem(f"{which}_rstd"), n)
                for t in range(ST):
                    last = dve.bn_stats(stats[:, t, :], src(t))
                link(last)
                for t in range(ST):
                    last = dve.bn_aggr(mean_var[which][:, t, :], stats[:, t, :])
                last.then_inc(sem(f"{which}_var"), 1)

            def ln_apply(which, n, src, dst):
                dve.wait_ge(sem(f"{which}_rstd"), n + 1)
                for t in range(ST):
                    last = dve.tensor_scalar(dst(t), src(t), mean_var[which][:, t, 0:1], rstd[which][:, t:t + 1],
                                             ALU.subtract, ALU.mult)
                last.then_inc(sem(which), 1)

            def split(w):
                dve.wait_ge(sem("split_hi"), w + 1)
                rest_of((wql, wkl, wvl, wol)[w][:, :, :], raw[w], (wqh, wkh, wvh, woh)[w][:, :, :])\
                    .then_inc(sem("split_lo"), 1)

            def ln1_stats(b):
                dve.wait_ge(sem(f"x_in{ring3(b)}"), 16 * (b // 3 + 1))
                ln_stats("ln1", b, lambda t: xin[:, ring3(b), t, :])

            def ln1(b):
                if b >= 1:
                    dve.wait_ge(sem("xt"), b)
                ln_apply("ln1", b, lambda t: xin[:, ring3(b), t, :], lambda t: xn[:, t, :])

            def xt(b):
                dve.wait_ge(sem("xt_hi"), b + 1)
                rest_of(xtl[:, b % 2, :, :], work_bank("xt", b).rearrange("p (k s) -> p k s", k=DC),
                        xth[:, b % 2, :, :]).then_inc(sem("xt_lo"), 1)

            def q(n):
                dve.wait_ge(sem("q_hi"), n + 1)
                dve.scalar_tensor_tensor(ql[:, n % 2, :, :], work_bank("q", n).rearrange("p (c s) -> p c s", c=2),
                                         SCALE, qh[:, n % 2, :, :].bitcast(F32), ALU.mult, ALU.subtract)\
                   .then_inc(sem("q_lo"), 1)

            def k(n):
                dve.wait_ge(sem("k_hi"), n + 1)
                if n == 0:
                    dve.wait_ge(sem("kzero"), 4)
                src = work_bank("k", n).rearrange("p (c s) -> p c s", c=2)
                for h in range(2):
                    r = slice(h * HD, (h + 1) * HD)
                    last = rest_of(kl[r, n % 2, :, h, :], src[r, :, :], kh[r, n % 2, :, h, :])
                last.then_inc(sem("k_lo"), 1)

            def scores(i):
                for qb in range(ST):
                    dve.wait_ge(sem("scores"), 2 * i + qb + 1)
                    dve.tensor_reduce(negmax[:, i % 2, qb, :], psum[:, qb, :].rearrange("p (h s) -> p h s", h=2),
                                      AX.X, ALU.max, negate=True).then_inc(sem("max"), 1)

            def norm(i, qb):
                dve.wait_ge(sem("exp"), 2 * i + qb + 1)
                link(dve.reciprocal(invtot[:, i % 2, qb, :], total[:, i % 2, qb, :]))
                for h in range(2):
                    last = dve.tensor_scalar(prob[:, i % 2, qb, h, :], prob[:, i % 2, qb, h, :],
                                             invtot[:, i % 2, qb, h:h + 1], None, ALU.mult)
                last.then_inc(sem("norm"), 1)

            def pv(i):
                b, c = divmod(i, PAIRS)
                dve.wait_ge(sem("a_hi"), i + 1)
                rest_of(al[:, b % 2, c, :], psum[:, 4 + i % 2, 0:S], ah[:, b % 2, c, :]).then_inc(sem("a_lo"), 1)

            def o(n):
                b, t = divmod(n, ST)
                dve.wait_ge(sem("o"), n + 1)
                if t == 0:
                    dve.wait_ge(sem("residual"), ST * (b + 1))
                    if b >= 2:
                        dve.wait_ge(sem(f"x2_out{b % 2}"), 16 * (b // 2))
                dve.tensor_tensor(x2[:, b % 2, t, :], work_bank("o", n)[:, 0:D], xin[:, ring3(b), t, :], ALU.add)\
                   .then_inc(sem("x2"), 1)

            def ln2_stats(b):
                dve.wait_ge(sem("x2"), ST * (b + 1))
                ln_stats("ln2", b, lambda t: x2[:, b % 2, t, :])

            def ln2(b):
                if b >= 2:
                    dve.wait_ge(sem("scatter"), 16 * 2 * ST * (b - 1))
                ln_apply("ln2", b, lambda t: x2[:, b % 2, t, :], lambda t: row[:, b % 2, t, 0:D])

            def logits(b):
                dve.wait_ge(sem("logits"), b + 1)
                if b == 0:
                    dve.wait_ge(sem("const_in"), 48)
                dve.tensor_tensor(logit[:, :, :], work_bank("logits", b)[:, 0:ST * NE]
                                  .rearrange("p (t e) -> p t e", t=ST),
                                  rb_all[:, :].unsqueeze(1).to_broadcast([P, ST, NE]), ALU.add)\
                   .then_inc(sem("biased"), 1)
                dve.wait_ge(sem("biased"), b + 1)
                link(dve.tensor_reduce(lmax[:, :], logit[:, :, :], AX.X, ALU.max))
                dve.tensor_tensor(logit[:, :, :], logit[:, :, :], lmax[:, :].unsqueeze(2).to_broadcast([P, ST, NE]),
                                  ALU.subtract).then_inc(sem("shifted"), 1)

            def gate(b):
                dve.wait_ge(sem("gate_exp"), b + 1)
                link(dve.tensor_reduce(lsum[:, :], lexp[:, :, :], AX.X, ALU.add))
                link(dve.reciprocal(linv[:, :], lsum[:, :]))
                link(dve.tensor_tensor(gates[:, :, :], lexp[:, :, :],
                                       linv[:, :].unsqueeze(2).to_broadcast([P, ST, NE]), ALU.mult))
                shape = [P, ST, NE, NE]
                other = gates[:, :, :].unsqueeze(2).to_broadcast(shape)
                own = gates[:, :, :].unsqueeze(3).to_broadcast(shape)
                for t in range(ST):
                    dve.tensor_tensor(above[:, t], other[:, t], own[:, t], ALU.is_gt)
                    last = dve.tensor_tensor(equal[:, t], other[:, t], own[:, t], ALU.is_equal)
                link(last)
                link(dve.tensor_tensor(equal[:, :, :, :], equal[:, :, :, :],
                                       lower[:, :, :].unsqueeze(1).to_broadcast(shape), ALU.mult))
                link(dve.tensor_tensor(above[:, :, :, :], above[:, :, :, :], equal[:, :, :, :], ALU.add))
                link(dve.tensor_reduce(rank[:, :, :], above[:, :, :, :], AX.X, ALU.add))
                dve.tensor_scalar(chosen[:, :, :], rank[:, :, :], 2.0, None, ALU.is_lt).then_inc(sem("chosen"), 1)

            def slot_(b):
                dve.wait_ge(sem("pos"), b + 1)
                if b >= 2:
                    dve.wait_ge(sem("scatter"), 16 * 2 * ST * (b - 1))
                count = work_bank("pos", b)[:, 0:ST * NE].rearrange("p (t e) -> p t e", t=ST)
                dve.tensor_tensor(slot[:, :, :], count, slot0[:, :].unsqueeze(1).to_broadcast([P, ST, NE]), ALU.add)
                dve.scalar_tensor_tensor(valid[:, :, :], count, float(CAP), chosen[:, :, :], ALU.is_le, ALU.mult)\
                   .then_inc(sem("slots"), 1)
                dve.wait_ge(sem("slots"), b + 1)
                for t in range(ST):
                    link(dve.tensor_tensor(before[:, :], before[:, :], chosen[:, t, :], ALU.add))
                dve.tensor_tensor(row[:, b % 2, :, GATE:ROW], gates[:, :, :], valid[:, :, :], ALU.mult)
                dve.tensor_scalar(row[:, b % 2, :, ID], tok[:, :], float(b * S), None, ALU.add)
                dve.scalar_tensor_tensor(lowkey[:, :, :], slot[:, :, :], -BIG, valid[:, :, :], ALU.add, ALU.mult)
                link(dve.scalar_tensor_tensor(highkey[:, :, :], slot[:, :, :], 1.0, valid[:, :, :], ALU.add, ALU.mult))
                dve.tensor_reduce(pick[:, 0, :], lowkey[:, :, :], AX.X, ALU.min)
                link(dve.tensor_reduce(pick[:, 1, :], highkey[:, :, :], AX.X, ALU.max))
                dve.tensor_scalar(pick[:, 0, :], pick[:, 0, :], BIG, None, ALU.add)
                link(dve.tensor_scalar(pick[:, 1, :], pick[:, 1, :], -1.0, None, ALU.add))
                link(dve.tensor_tensor(same[:, 0, :], pick[:, 1, :], pick[:, 0, :], ALU.is_le))
                link(dve.scalar_tensor_tensor(pick[:, 1, :], same[:, 0, :], BIG, pick[:, 1, :], ALU.mult, ALU.add))
                dve.tensor_copy(picki[:, b % 2, :, :], pick[:, :, :]).then_inc(sem("picks"), 1)

            steps = dict(split=split, ln1=ln1, xt=xt, q=q, k=k, scores=scores, norm0=lambda i: norm(i, 0), norm1=lambda i: norm(i, 1), pv=pv, o=o,
                         ln1_stats=ln1_stats, ln2_stats=ln2_stats, ln2=ln2, logits=logits, gate=gate, slot=slot_)
            for stage, n in TIMELINE:
                if stage in steps:
                    steps[stage](n)

            def split_w(e, part):
                r = e % 2
                dve.wait_ge(sem("wsplit_hi"), 2 * e + part + 1)
                rest_of((w1l, w2l)[part][r][:, :, :], (w1r, w2r)[part][:, :, :], (w1h, w2h)[part][r][:, :, :])\
                    .then_inc(sem("wsplit_lo"), 1)

            def turn_rows(e):
                for u in range(3):
                    at, s0, s1 = 3 * e + u, 2 * u, min(2 * u + 2, ET)
                    dve.wait_ge(sem("buf_hi"), at + 1)
                    for kk in range(DC):
                        src = psum[:, 6 + at % 2, :].rearrange("p (s k c) -> p k s c", k=DC, c=P)
                        part = lambda a: a[:, e % 2, kk, s0 * P:s1 * P].rearrange("p (s c) -> p s c", c=P)
                        last = rest_of(part(bufl), src[:, kk, 0:s1 - s0, :], part(bufh))
                    last.then_inc(sem("buf_lo"), 1)
                if e >= 2:
                    dve.wait_ge(sem("added"), 16 * ET * (e - 1))
                dve.tensor_copy(rowi[:, e % 2, :], rows[:, e % 2, :, ID]).then_inc(sem("rowi"), 1)

            def split_hid(at):
                j = at % HC
                dve.wait_ge(sem("gelu"), at + 1)
                if j == 0 and at:
                    dve.wait_ge(sem("down"), ET * (at // HC))
                dve.tensor_copy(hidh[:, j, :], hid[:, at % 2, :]).then_inc(sem("hid_hi"), 1)
                dve.wait_ge(sem("hid_hi"), at + 1)
                rest_of(hidl[:, j, :], hid[:, at % 2, :], hidh[:, j, :]).then_inc(sem("hid_lo"), 1)

            def weigh(e, s):
                dve.wait_ge(sem("down"), ET * e + s + 1)
                if e >= 2 and s == 0:
                    dve.wait_ge(sem("added"), 16 * ET * (e - 1))
                link(dve.tensor_tensor(y[:, e % 2, s, :], psum[:, 4 + (ET * e + s) % 2, 0:D], b2_all[:, e, :], ALU.add))
                dve.tensor_scalar(y[:, e % 2, s, :], y[:, e % 2, s, :], rows[:, e % 2, s, GATE + e:GATE + e + 1],
                                  None, ALU.mult).then_inc(sem("y"), 1)

            split_w(0, 0)
            split_w(0, 1)
            dve.wait_ge(sem("rows_in0"), 16)
            turn_rows(0)
            for e in range(NE):
                for j in range(HC):
                    split_hid(HC * e + j)
                    if e + 1 < NE and j in (3, 6):
                        split_w(e + 1, (j - 3) // 3)
                if e == 0:
                    dve.wait_ge(sem("b2_in"), 16)
                if e + 1 < NE:
                    dve.wait_ge(sem(f"rows_in{(e + 1) % 2}"), 16 * ((e + 1) // 2 + 1))
                    turn_rows(e + 1)
                for s in range(ET):
                    weigh(e, s)


def kernel(x, ctx_768, L0_xattn_w_q, L0_xattn_w_k, L0_xattn_w_v, L0_xattn_w_o, L0_xattn_b_o,
           L0_ffn_router_w, L0_ffn_router_b, L0_ffn_w1, L0_ffn_b1, L0_ffn_w2, L0_ffn_b2):
    import numpy as np
    import concourse.bacc as bacc
    from concourse.bass_utils import run_bass_kernel_spmd as run

    ins = {
        "x": x,
        "ctxt": np.asarray(ctx_768).reshape(N, CD).T,
        "wq": L0_xattn_w_q, "wk": L0_xattn_w_k, "wv": L0_xattn_w_v, "wo": L0_xattn_w_o, "bo": L0_xattn_b_o,
        "rw": L0_ffn_router_w, "rb": L0_ffn_router_b, "w1": L0_ffn_w1,
        "b1": np.asarray(L0_ffn_b1).reshape(NE, HC, P).transpose(2, 0, 1),
        "w2": L0_ffn_w2, "b2": L0_ffn_b2,
    }
    nc = bacc.Bacc("TRN2", target_bir_lowering=False, num_devices=1)
    arrays, args = {}, []
    for name, a in ins.items():
        a = np.ascontiguousarray(a)
        arrays[f"in_{name}"] = a
        args.append(nc.dram_tensor(f"in_{name}", a.shape, F32, kind="ExternalInput").ap())
    args.append(nc.dram_tensor("out_rows", (N + CAP, D), F32, kind="ExternalOutput").ap())
    build(nc, *args)
    r = run(nc, [arrays], core_ids=[0])
    return r.results[0]["out_rows"][:N].reshape(B, S, D)
```

```python
from contextlib import ExitStack

import concourse.bass as bass
from concourse import mybir

F32 = mybir.dt.float32
F32R = mybir.dt.float32r
BF16 = mybir.dt.bfloat16
I32 = mybir.dt.int32
ALU = mybir.AluOpType
ACT = mybir.ActivationFunctionType
AX = mybir.AxisListType

P = 128
B, S, D = 16, 256, 256
CD = 192
HD = 64
INNER = 1024
PAIRS = INNER // P
ST = S // P
DC = D // P
NE, HID = 8, 1024
HC = HID // P
N = B * S
CAP = -(-N * 5 // (NE * 4))
ET = CAP // P
EPS = 1e-5
SCALE = HD ** -0.5
BIG = 65536.0
ID, GATE = D, D + 1
ROW = D + 1 + NE
HALF = CAP // 2
STEPS = B * PAIRS
TURNS = -(-ET // 2)
TURN_AFTER = (3, 5, 7)
WSPLITS = 4
SPLITS = [(0, 0), (1, 0), (2, 0), (0, 1), (1, 1), (2, 1), (3, 0), (3, 1)]
assert len(TURN_AFTER) == TURNS and WSPLITS <= ET
assert CAP == ET * P and CAP % 2 == 0 and HALF <= 512


def timeline():
    out = [("ln1_stats", 0), ("ctx", 0), ("split", 0), ("ln1", 0), ("split", 1), ("xt", 0), ("q", 0), ("k", 0),
           ("split", 2), ("split", 3)]
    for i in range(STEPS + PAIRS):
        b, c = divmod(i, PAIRS)
        item = i // 2 + 1
        if i < STEPS:
            out += [("scores", i)]
        if 1 <= i <= STEPS:
            out += [("norm0", i - 1), ("norm1", i - 1)]
        if item < STEPS // 2:
            out += [("k" if i % 2 == 0 else "q", item)]
        if i < STEPS:
            out += [("exp1", i)]
        if 2 <= i < STEPS + 2:
            out += [("pv", i - 2)]
        if b == 0:
            out += {0: [("v", 0), ("v", 1), ("ln1_stats", 1), ("ctx", 1), ("split", 4)],
                    1: [("split", 5), ("split", 6), ("split", 7), ("ln1", 1)],
                    2: [("v", 2), ("xt", 1)],
                    3: [("v", 3)]}.get(c, [])
        if b + 1 < B:
            v_at = (1, 2, 5, 7) if b else (3, 4, 5, 7)
            if c == 0 and b:
                out += [("xt", b + 1)]
            if c in v_at:
                out += [("v", 4 * (b + 1) + v_at.index(c))]
        if 0 <= b - 1 < B - 1:
            out += {3: [("o", ST * (b - 1))], 4: [("o", ST * (b - 1) + 1), ("ln2_stats", b - 1)],
                    5: [("ln2", b - 1)], 6: [("x2t", b - 1)], 7: [("logits", b - 1)]}.get(c, [])
        if 0 <= b - 2 < B - 1:
            out += {0: [("gate", b - 2)], 1: [("rank", b - 2)], 2: [("pos", b - 2), ("slot", b - 2)],
                    3: [("pick", b - 2)]}.get(c, [])
        if b + 2 < B:
            out += {5: [("ln1_stats", b + 2)], 6: [("ln1", b + 2), ("ctx", b + 2)]}.get(c, [])
        if 1 <= i <= STEPS:
            out += [("turn", i - 1)]
    out += [("o", ST * B - 2), ("o", ST * B - 1)]
    out += [(stage, B - 1) for stage in ("ln2_stats", "ln2", "x2t", "logits", "gate", "rank", "pos", "slot", "pick")]
    return out


TIMELINE = timeline()
WORK_BANKS = 3
WORKS = [(s, n) for s, n in TIMELINE if s in ("xt", "q", "k", "v", "o", "x2t", "logits", "pos")]
WORK_READ = {"xt": "xt_lo", "q": "q_lo", "k": "k_lo", "v": "v_sb", "o": "x2", "x2t": "x2t_sb",
             "logits": "biased", "pos": "slots"}


def w_piece(w, cut):
    n = w.shape[1] // (WSPLITS // 2)
    return w[:, cut * n:(cut + 1) * n, :]


def build(nc, x, ctxt, wq, wk, wv, wo, bo, rw, rb, w1, b1, w2, b2, out_rows):
    es = ExitStack()
    with es:
        sems = {}

        def sem(name):
            if name not in sems:
                sems[name] = es.enter_context(nc.semaphore("s_" + name))
            return sems[name]

        def sb(stack, name, shape, dt=F32):
            return stack.enter_context(nc.sbuf_tensor(name, [P, *shape], dt))

        psum = es.enter_context(nc.psum_tensor("psum", [P, 8, 512], F32))
        table = nc.dram_tensor("slot_table", [NE * CAP, ROW], F32, kind="Internal").ap()

        ident = sb(es, "ident", [P])
        b1t = sb(es, "b1t", [NE, HC])
        first = ExitStack()
        wqh, wql = (sb(first, n, [DC, INNER], F32R) for n in ("wqh", "wql"))
        wkh, wkl = (sb(first, n, [2, INNER], F32R) for n in ("wkh", "wkl"))
        wvh, wvl = (sb(first, n, [2, INNER], F32R) for n in ("wvh", "wvl"))
        rest = ExitStack()
        woh, wol = (sb(rest, n, [PAIRS, D], F32R) for n in ("woh", "wol"))
        xin = sb(rest, "xin", [3, ST, D])
        xn = sb(rest, "xn", [ST, D])
        xth, xtl = (sb(rest, n, [2, DC, S], F32R) for n in ("xth", "xtl"))
        c0 = sb(rest, "c0", [2, S])
        c1 = sb(rest, "c1", [2, S])
        c0h, c0l = (sb(rest, n, [2, S], F32R) for n in ("c0h", "c0l"))
        c1s = sb(rest, "c1s", [2, S], F32R)
        c1t = sb(rest, "c1t", [S], F32R)
        qh, ql = (sb(rest, n, [2, 2, S], F32R) for n in ("qh", "ql"))
        kh, kl = (sb(rest, n, [2, 2, 2, S], F32R) for n in ("kh", "kl"))
        v = sb(rest, "v", [2, ST, INNER])
        prob = sb(rest, "prob", [3, 2, 2, S])
        probt = sb(rest, "probt", [2, 2, ST, S])
        ah, al = (sb(rest, n, [2, PAIRS, S], F32R) for n in ("ah", "al"))
        x2 = sb(rest, "x2", [2, ST, D])
        row = sb(rest, "row", [2, ST, ROW])
        x2t = sb(rest, "x2t", [DC, S])
        blank = sb(rest, "blank", [ET, ROW])
        bo_all = sb(rest, "bo_all", [D])
        rwt = sb(rest, "rwt", [DC, NE])
        rb_all = sb(rest, "rb_all", [NE])
        upto = sb(rest, "upto", [P], BF16)
        ones = sb(rest, "ones", [P], BF16)
        lower = sb(rest, "lower", [NE, NE])
        slot0i = sb(rest, "slot0i", [NE], I32)
        slot0 = sb(rest, "slot0", [NE])
        toki = sb(rest, "toki", [ST], I32)
        tok = sb(rest, "tok", [ST])
        dumpi = sb(rest, "dumpi", [ET], I32)
        negmax = sb(rest, "negmax", [2, 2, 2])
        total = sb(rest, "total", [2, 2, 2])
        invtot = sb(rest, "invtot", [2, 2, 2])
        stats = sb(rest, "stats", [ST, 6])
        mean_var = {n: sb(rest, n + "_mean_var", [ST, 2]) for n in ("ln1", "ln2")}
        rstd = {n: sb(rest, n + "_rstd", [ST]) for n in ("ln1", "ln2")}
        shifted, newton, power = (sb(rest, n, [ST]) for n in ("shifted", "newton", "power"))
        logit, lexp, gates = (sb(rest, n, [ST, NE]) for n in ("logit", "lexp", "gates"))
        lmax, lsum, linv = (sb(rest, n, [ST]) for n in ("lmax", "lsum", "linv"))
        above, equal = (sb(rest, n, [ST, NE, NE]) for n in ("above", "equal"))
        rank, slot, valid, lowkey, highkey = (sb(rest, n, [ST, NE])
                                              for n in ("rank", "slot", "valid", "lowkey", "highkey"))
        chosen = sb(rest, "chosen", [ST, NE], BF16)
        before = sb(rest, "before", [NE], BF16)
        pick, same = (sb(rest, n, [2, ST]) for n in ("pick", "same"))
        picki = sb(rest, "picki", [2, 2, ST], I32)
        rest.close()
        first.close()
        late = es.enter_context(ExitStack())
        w1r, w2r = sb(late, "w1r", [DC, HID]), sb(late, "w2r", [HC, D])
        w1h, w1l, w2h, w2l = [], [], [], []
        for r in range(2):
            w1h.append(sb(late, f"w1h{r}", [DC, HID], F32R))
            w1l.append(sb(late, f"w1l{r}", [DC, HID], F32R))
            w2h.append(sb(late, f"w2h{r}", [HC, D], F32R))
            w2l.append(sb(late, f"w2l{r}", [HC, D], F32R))
        hidh, hidl = (sb(late, n, [HC, CAP], F32R) for n in ("hidh", "hidl"))
        hid = sb(late, "hid", [2, CAP])
        bufh, bufl = (sb(late, n, [2, DC, CAP], F32R) for n in ("bufh", "bufl"))
        rows = sb(late, "rows", [2, ET, ROW])
        rowi = sb(late, "rowi", [2, ET], I32)
        y = sb(late, "y", [2, ET, D])
        b2_all = sb(late, "b2_all", [NE, D])

        flat = lambda t: t.rearrange("p a b s -> p (a b s)")
        raw = [v[:, 0, 0, :], v[:, 0, 1, :], flat(prob[:, 1, :, :, :]), flat(probt[:, 0, :, :, :]),
               v[:, 1, 0, :], v[:, 1, 1, :], flat(prob[:, 2, :, :, :]), flat(probt[:, 1, :, :, :])]

        def pieces(at):
            which, half = SPLITS[at]
            if which == 3:
                part = slice(half * PAIRS // 2, (half + 1) * PAIRS // 2)
                return raw[at].rearrange("p (k n) -> p k n", k=PAIRS // 2), woh[:, part, :], wol[:, part, :]
            cols = slice(half * 512, (half + 1) * 512)
            return (raw[at].rearrange("p (k n) -> p k n", k=2), (wqh, wkh, wvh)[which][:, :, cols],
                    (wql, wkl, wvl)[which][:, :, cols])

        block = es.enter_context(nc.Block())

        def all_stored(eng):
            eng.wait_ge(sem("spare_clear"), 16)
            for r in range(2):
                eng.wait_ge(sem(f"x2_out{r}"), 16 * B // 2)

        ring3 = lambda n: n % 3

        @block.sync
        def _(sp):
            def load_x(b):
                if b >= 3:
                    sp.wait_ge(sem("x2"), ST * (b - 2))
                sp.dma_start(xin[:, ring3(b), :, :], x[b].rearrange("(t p) d -> p t d", p=P))\
                  .then_inc(sem(f"x_in{ring3(b)}"), 16)

            def load_ctx(b):
                if b >= 2:
                    sp.wait_ge(sem("ctx"), b - 1)
                cols = slice(b * S, (b + 1) * S)
                sp.dma_start(c0[:, b % 2, :], ctxt[0:P, cols]).then_inc(sem(f"ctx_in{b % 2}"), 16)
                for h in range(2):
                    sp.dma_start(c1[h * HD:(h + 1) * HD, b % 2, :], ctxt[P:CD, cols])\
                      .then_inc(sem(f"ctx_in{b % 2}"), 16)

            def load_piece(at):
                which, half = SPLITS[at]
                w, cols = (wq, wk, wv, wo)[which], slice(half * 512, (half + 1) * 512)
                dst = pieces(at)[0]
                if which == 0:
                    sp.dma_start(dst, w[:, cols].rearrange("(k p) n -> p k n", p=P)).then_inc(sem(f"w_in{at}"), 16)
                elif which == 3:
                    sp.dma_start(dst, w[cols, :].rearrange("(k p) n -> p k n", p=P)).then_inc(sem(f"w_in{at}"), 16)
                else:
                    sp.dma_start(dst[:, 0, :], w[0:P, cols]).then_inc(sem(f"w_in{at}"), 16)
                    for h in range(2):
                        sp.dma_start(dst[h * HD:(h + 1) * HD, 1, :], w[P:CD, cols]).then_inc(sem(f"w_in{at}"), 16)

            load_x(0)
            load_ctx(0)
            for at in range(3):
                load_piece(at)
            sp.dma_start(bo_all[:, :], bo.partition_broadcast(P)).then_inc(sem("const_in"), 16)
            load_piece(3)
            load_piece(4)
            load_x(1)
            load_ctx(1)
            for at in range(5, 8):
                load_piece(at)
            load_x(2)
            sp.dma_start(rb_all[:, :], rb.partition_broadcast(P)).then_inc(sem("const_in"), 16)
            sp.dma_start(rwt[:, :, :], rw.rearrange("(k p) n -> p k n", p=P)).then_inc(sem("const_in"), 16)
            sp.dma_start(b1t[:, :, :], b1).then_inc(sem("b1_in"), 16)
            sp.wait_ge(sem("blank"), 1)
            for e in range(NE):
                sp.dma_start(table[e * CAP:(e + 1) * CAP, :].rearrange("(s p) w -> p s w", p=P),
                             blank[:, :, :]).then_inc(sem("table_clear"), 16)
            sp.dma_start(out_rows[N:N + CAP, :].rearrange("(s p) w -> p s w", p=P),
                         blank[:, :, 0:D]).then_inc(sem("spare_clear"), 16)
            for b in range(B):
                if b + 2 < B:
                    load_ctx(b + 2)
                if b + 3 < B:
                    load_x(b + 3)
                sp.wait_ge(sem("x2"), ST * (b + 1))
                sp.dma_start(out_rows[b * S:(b + 1) * S, :].rearrange("(t p) d -> p t d", p=P),
                             x2[:, b % 2, :, :]).then_inc(sem(f"x2_out{b % 2}"), 16)

            sp.wait_ge(sem("q"), STEPS // 2)
            sp.wait_ge(sem("k"), STEPS // 2)
            sp.wait_ge(sem("v"), 4 * B)

            def load_w(e):
                if e >= 1:
                    sp.wait_ge(sem("wsplit_hi"), WSPLITS * e)
                    sp.wait_ge(sem("wsplit_lo"), WSPLITS * e)
                sp.dma_start(w1r[:, :, :], w1[e].rearrange("(k p) n -> p k n", p=P)).then_inc(sem("w1_in"), 16)
                sp.dma_start(w2r[:, :, :], w2[e].rearrange("(k p) n -> p k n", p=P)).then_inc(sem("w2_in"), 16)

            def load_rows(e):
                if e >= 2:
                    sp.wait_ge(sem("y"), ET * (e - 1))
                sp.dma_start(rows[:, e % 2, :, :],
                             table[e * CAP:(e + 1) * CAP, :].rearrange("(s p) w -> p s w", p=P))\
                  .then_inc(sem(f"rows_in{e % 2}"), 16)

            load_w(0)
            sp.wait_ge(sem("scatter"), 16 * 2 * ST * B)
            all_stored(sp)
            load_rows(0)
            sp.dma_start(b2_all[:, :, :], b2.partition_broadcast(P)).then_inc(sem("b2_in"), 16)
            load_rows(1)
            for e in range(1, NE):
                load_w(e)
                if e + 1 < NE:
                    load_rows(e + 1)
            sp.wait_ge(sem("added"), 16 * ET * NE)

        @block.gpsimd
        def _(pool):
            done = [0]

            def link(ins):
                done[0] += 1
                ins.then_inc(sem("pool"), 1)
                pool.wait_ge(sem("pool"), done[0])

            def link_as(name, ins):
                ins.then_inc(sem(name), 1)
                told[name] = told.get(name, 0) + 1
                pool.wait_ge(sem(name), told[name])

            told = {}

            link(pool.memset(power[:, :], -0.5))
            link(pool.memset(ident[:, :], 0.0))
            link_as("ident", pool.affine_select(out=ident[:, :], in_=ident[:, :], compare_op=ALU.not_equal,
                                                fill=1.0, base=0, pattern=[[-1, P]], channel_multiplier=1))
            link_as("kzero", pool.memset(kh[HD:P, :, :, 0, :].bitcast(F32), 0.0))
            link_as("kzero", pool.memset(kh[0:HD, :, :, 1, :].bitcast(F32), 0.0))

            def ctx(b):
                p = b % 2
                pool.wait_ge(sem(f"ctx_in{p}"), 48 * (b // 2 + 1))
                if b >= 2:
                    pool.wait_ge(sem("k"), 4 * (b - 1))
                    pool.wait_ge(sem("v"), 4 * (b - 1))
                link(pool.tensor_copy(c1s[0:HD, p, :], c1[0:HD, p, :]))
                link(pool.tensor_copy(c1t[HD:P, :], c1[HD:P, p, :]))
                link(pool.tensor_copy(c0h[:, p, :], c0[:, p, :]))
                link(pool.tensor_tensor(c1s[HD:P, p, :], c1[HD:P, p, :], c1t[HD:P, :].bitcast(F32), ALU.subtract))
                link_as("ctx", pool.tensor_tensor(c0l[:, p, :], c0[:, p, :], c0h[:, p, :].bitcast(F32),
                                                  ALU.subtract))

            def inverse_root(which, n):
                pool.wait_ge(sem(f"{which}_var"), n + 1)
                if n >= 1:
                    pool.wait_ge(sem(which), n)
                root = rstd[which][:, :]
                link(pool.tensor_scalar(shifted[:, :], mean_var[which][:, :, 1], EPS, None, ALU.add))
                link(pool.tensor_tensor(root, shifted[:, :], power[:, :], ALU.pow))
                link(pool.tensor_tensor(newton[:, :], root, root, ALU.mult))
                link(pool.tensor_tensor(newton[:, :], newton[:, :], shifted[:, :], ALU.mult))
                link(pool.tensor_scalar(newton[:, :], newton[:, :], -0.5, 1.5, ALU.mult, ALU.add))
                link_as(f"{which}_rstd", pool.tensor_tensor(root, root, newton[:, :], ALU.mult))

            def ln1(b):
                pool.wait_ge(sem("const_in"), 48)
                pool.wait_ge(sem("ln1"), b + 1)
                for t in range(ST):
                    link_as("residual", pool.tensor_tensor(xin[:, ring3(b), t, :], xin[:, ring3(b), t, :],
                                                           bo_all[:, :], ALU.add))

            def constants():
                link(pool.memset(upto[:, :], 1.0))
                link(pool.affine_select(out=upto[:, :], in_=upto[:, :], compare_op=ALU.is_ge, fill=0.0, base=0,
                                        pattern=[[1, P]], channel_multiplier=-1))
                link(pool.memset(ones[:, :], 1.0))
                link(pool.memset(before[:, :], 0.0))
                link(pool.memset(lower[:, :, :], 1.0))
                link(pool.affine_select(out=lower[:, :, :], in_=lower[:, :, :], compare_op=ALU.is_gt, fill=0.0,
                                        base=0, pattern=[[1, NE], [-1, NE]], channel_multiplier=0))
                link(pool.iota(slot0i[:, :], pattern=[[CAP, NE]], base=-1, channel_multiplier=0))
                link(pool.iota(dumpi[:, :], pattern=[[P, ET]], base=N, channel_multiplier=1))
                link(pool.iota(toki[:, :], pattern=[[P, ST]], base=0, channel_multiplier=1))
                link(pool.tensor_copy(slot0[:, :], slot0i[:, :]))
                link(pool.tensor_copy(tok[:, :], toki[:, :]))
                link(pool.memset(blank[:, :, :], 0.0))
                link_as("blank", pool.tensor_copy(blank[:, :, ID], dumpi[:, :]))

            def slots(b):
                if b == 0:
                    pool.wait_ge(sem("table_clear"), 16 * NE)
                pool.wait_ge(sem("picks"), b + 1)
                for k in range(2):
                    for t in range(ST):
                        pool.indirect_dma_start(
                            out=table, out_offset=bass.IndirectOffsetOnAxis(ap=picki[:, b % 2, k, t:t + 1], axis=0),
                            in_=row[:, b % 2, t, :], in_offset=None, bounds_check=NE * CAP - 1,
                            oob_is_err=False).then_inc(sem("scatter"), 16)
                pool.wait_ge(sem("scatter"), 16 * 2 * ST * (b + 1))

            for stage, n in TIMELINE:
                if stage == "ctx":
                    ctx(n)
                if stage in ("ln1_stats", "ln2_stats"):
                    inverse_root(stage[:3], n)
                if stage == "ln1":
                    if n == 1:
                        constants()
                    ln1(n)
                if stage == "pick":
                    slots(n)

            all_stored(pool)
            for e in range(NE):
                pool.wait_ge(sem("rowi"), e + 1)
                if e >= 1:
                    pool.wait_ge(sem("added"), 16 * ET * e)
                for s in range(ET):
                    pool.wait_ge(sem("y"), ET * e + s + 1)
                    pool.indirect_dma_start(
                        out=out_rows, out_offset=bass.IndirectOffsetOnAxis(ap=rowi[:, e % 2, s:s + 1], axis=0),
                        in_=y[:, e % 2, s, :], in_offset=None, bounds_check=N + CAP - 1, oob_is_err=True,
                        compute_op=ALU.add).then_inc(sem("added"), 16)

        @block.tensor
        def _(pe):
            work = {w: n for n, w in enumerate(WORKS)}

            def bank(stage, n):
                at = work[stage, n]
                if at >= WORK_BANKS:
                    s, m = WORKS[at - WORK_BANKS]
                    pe.wait_ge(sem(WORK_READ[s]), m + 1)
                return psum[:, 5 + at % WORK_BANKS, :]

            def products(dst, terms):
                for j, (lhs, rhs) in enumerate(terms):
                    mm = pe.matmul(dst, lhs, rhs, start=(j == 0), stop=(j == len(terms) - 1))
                return mm

            def xt(b):
                dst = bank("xt", b)
                pe.wait_ge(sem("ln1"), b + 1)
                for k in range(DC):
                    for t in range(ST):
                        mm = pe.transpose(dst[:, k * S + t * P:k * S + (t + 1) * P],
                                          xn[:, t, k * P:(k + 1) * P], ident[:, :])
                mm.then_inc(sem("xt"), 1)

            def q(n):
                b, dst = n // 4, bank("q", n)
                pe.wait_ge(sem("xt_lo"), b + 1)
                if n in (0, 2):
                    pe.wait_ge(sem("split_lo"), 1 if n == 0 else 4)
                for cc in range(2):
                    cols = slice((n % 4 * 2 + cc) * P, (n % 4 * 2 + cc + 1) * P)
                    mm = products(dst[:, cc * S:(cc + 1) * S],
                                  [(w[:, k, cols], a[:, b % 2, k, :]) for k in range(DC)
                                   for w, a in ((wqh, xth), (wqh, xtl), (wql, xth))])
                mm.then_inc(sem("q"), 1)

            def k(n):
                b, dst = n // 4, bank("k", n)
                pe.wait_ge(sem("ctx"), b + 1)
                if n in (0, 2):
                    pe.wait_ge(sem("split_lo"), 2 if n == 0 else 5)
                for cc in range(2):
                    cols = slice((n % 4 * 2 + cc) * P, (n % 4 * 2 + cc + 1) * P)
                    mm = products(dst[:, cc * S:(cc + 1) * S],
                                  [(wkh[:, 0, cols], c0h[:, b % 2, :]), (wkh[:, 0, cols], c0l[:, b % 2, :]),
                                   (wkl[:, 0, cols], c0h[:, b % 2, :]), (wkh[:, 1, cols], c1s[:, b % 2, :]),
                                   (wkl[:, 1, cols], c1s[:, b % 2, :])])
                mm.then_inc(sem("k"), 1)

            def v_(n):
                b, half, t = n // 4, n % 4 // 2, n % 2
                dst = bank("v", n)
                pe.wait_ge(sem("ctx"), b + 1)
                if n in (0, 2):
                    pe.wait_ge(sem("split_lo"), 3 if n == 0 else 6)
                cols, tt = slice(half * 512, half * 512 + 512), slice(t * P, (t + 1) * P)
                products(dst, [(c0h[:, b % 2, tt], wvh[:, 0, cols]), (c0l[:, b % 2, tt], wvh[:, 0, cols]),
                               (c0h[:, b % 2, tt], wvl[:, 0, cols]), (c1s[:, b % 2, tt], wvh[:, 1, cols]),
                               (c1s[:, b % 2, tt], wvl[:, 1, cols])]).then_inc(sem("v"), 1)

            def scores(i):
                n, cc = i // 2, i % 2
                pe.wait_ge(sem("q_lo"), n + 1)
                pe.wait_ge(sem("k_lo"), n + 1)
                for qb in range(ST):
                    if i >= 1:
                        pe.wait_ge(sem("exp"), 2 * (i - 1) + qb + 1)
                    cols = slice(qb * P, (qb + 1) * P)
                    both = lambda t: t[:, n % 2, cc, :, :].rearrange("p h s -> p (h s)")
                    products(psum[:, qb, :],
                             [(qh[:, n % 2, cc, cols], both(kh)), (qh[:, n % 2, cc, cols], both(kl)),
                              (ql[:, n % 2, cc, cols], both(kh))]).then_inc(sem("scores"), 1)

            def turn(i):
                for h in range(2):
                    if i >= 1:
                        pe.wait_ge(sem("probt"), 2 * (i - 1) + h + 1)
                    for qb in range(ST):
                        pe.wait_ge(sem("norm"), 2 * i + qb + 1)
                        for kb in range(ST):
                            mm = pe.transpose(psum[:, 2 + h, kb * S + qb * P:kb * S + (qb + 1) * P],
                                              prob[:, i % 3, qb, h, kb * P:(kb + 1) * P], ident[:, :])
                    mm.then_inc(sem("turn"), 1)

            def pv(i):
                b, c = divmod(i, PAIRS)
                pe.wait_ge(sem("v_sb"), 4 * b + (2 if c < PAIRS // 2 else 4))
                pe.wait_ge(sem("a_lo"), i)
                pe.wait_ge(sem("probt"), 2 * (i + 1))
                for h in range(2):
                    for kb in range(ST):
                        cols = slice((2 * c + h) * HD, (2 * c + h + 1) * HD)
                        mm = pe.matmul(psum[h * HD:(h + 1) * HD, 4, 0:S], v[:, b % 2, kb, cols],
                                       probt[:, i % 2, h, kb, :], start=(kb == 0), stop=(kb == ST - 1))
                mm.then_inc(sem("pv"), 1)

            def o(n):
                b, t = divmod(n, ST)
                dst, tt = bank("o", n), slice(t * P, (t + 1) * P)
                pe.wait_ge(sem("a_lo"), PAIRS * (b + 1))
                if n == 0:
                    pe.wait_ge(sem("split_lo"), 8)
                products(dst[:, 0:D], [(a[:, b % 2, c, tt], w[:, c, :]) for c in range(PAIRS)
                                       for a, w in ((ah, woh), (ah, wol), (al, woh))]).then_inc(sem("o"), 1)

            def x2t_(b):
                dst = bank("x2t", b)
                pe.wait_ge(sem("ln2"), b + 1)
                for k in range(DC):
                    for t in range(ST):
                        mm = pe.transpose(dst[:, k * S + t * P:k * S + (t + 1) * P],
                                          row[:, b % 2, t, k * P:(k + 1) * P], ident[:, :])
                mm.then_inc(sem("x2t"), 1)

            def logits(b):
                dst = bank("logits", b)
                pe.wait_ge(sem("x2t_sb"), b + 1)
                for t in range(ST):
                    mm = products(dst[:, t * NE:(t + 1) * NE],
                                  [(x2t[:, k, t * P:(t + 1) * P], rwt[:, k, :]) for k in range(DC)])
                mm.then_inc(sem("logits"), 1)

            def pos(b):
                dst = bank("pos", b)
                pe.wait_ge(sem("chosen"), b + 1)
                products(dst[:, 0:NE], [(upto[:, :], chosen[:, 0, :]), (ones[:, :], before[:, :])])
                products(dst[:, NE:2 * NE], [(upto[:, :], chosen[:, 1, :]), (ones[:, :], chosen[:, 0, :]),
                                             (ones[:, :], before[:, :])]).then_inc(sem("pos"), 1)

            pe.wait_ge(sem("ident"), 1)
            steps = dict(xt=xt, q=q, k=k, v=v_, scores=scores, turn=turn, pv=pv, o=o, x2t=x2t_, logits=logits, pos=pos)
            for stage, n in TIMELINE:
                if stage in steps:
                    steps[stage](n)

            def turn_rows(e, u):
                pe.wait_ge(sem(f"rows_in{e % 2}"), 16 * (e // 2 + 1))
                at = TURNS * e + u
                if at >= 2:
                    pe.wait_ge(sem("buf_lo"), at - 1)
                for s in range(2 * u, min(2 * u + 2, ET)):
                    for kk in range(DC):
                        col = (s - 2 * u) * D + kk * P
                        mm = pe.transpose(psum[:, 6 + at % 2, col:col + P],
                                          rows[:, e % 2, s, kk * P:(kk + 1) * P], ident[:, :])
                mm.then_inc(sem("turn_rows"), 1)

            def up(e):
                r = e % 2
                pe.wait_ge(sem("buf_lo"), TURNS * (e + 1))
                pe.wait_ge(sem("wsplit_lo"), WSPLITS * e + WSPLITS // 2)
                for j in range(HC):
                    at = HC * e + j
                    if at >= 2:
                        pe.wait_ge(sem("gelu"), at - 1)
                    cols = slice(j * P, (j + 1) * P)
                    for half in range(2):
                        hs = slice(half * HALF, (half + 1) * HALF)
                        mm = products(psum[:, 2 * (at % 2) + half, 0:HALF],
                                      [(w[:, kk, cols], a[:, r, kk, hs]) for kk in range(DC)
                                       for w, a in ((w1h[r], bufh), (w1h[r], bufl), (w1l[r], bufh))])
                    mm.then_inc(sem("up"), 1)
                    if e + 1 < NE and j in TURN_AFTER:
                        turn_rows(e + 1, TURN_AFTER.index(j))

            def down(e):
                r = e % 2
                pe.wait_ge(sem("wsplit_lo"), WSPLITS * (e + 1))
                for s in range(ET):
                    at = ET * e + s
                    if at >= 2:
                        pe.wait_ge(sem("y"), at - 1)
                    ss = slice(s * P, (s + 1) * P)
                    dst = psum[:, 4 + at % 2, 0:D]
                    for j in range(HC):
                        if s == 0:
                            pe.wait_ge(sem("hid_lo"), HC * e + j + 1)
                        for m, (a, w) in enumerate(((hidh, w2h[r]), (hidh, w2l[r]), (hidl, w2h[r]))):
                            mm = pe.matmul(dst, a[:, j, ss], w[:, j, :], start=(j == 0 and m == 0),
                                           stop=(j == HC - 1 and m == 2))
                    mm.then_inc(sem("down"), 1)

            pe.wait_ge(sem("slots"), B)
            for u in range(TURNS):
                turn_rows(0, u)
            for e in range(NE):
                up(e)
                down(e)

        @block.scalar
        def _(act):
            copy = lambda dst, src, **kw: act.activation(dst, src, ACT.Copy, **kw)
            def work_bank(stage, n):
                return psum[:, 5 + WORKS.index((stage, n)) % WORK_BANKS, :]

            def split(w):
                act.wait_ge(sem(f"w_in{w}"), 48 if SPLITS[w][0] in (1, 2) else 16)
                whole, head, _ = pieces(w)
                copy(head, whole).then_inc(sem("split_hi"), 1)

            def xt(b):
                act.wait_ge(sem("xt"), b + 1)
                if b >= 2:
                    act.wait_ge(sem("q"), 4 * (b - 1))
                copy(xth[:, b % 2, :, :], work_bank("xt", b).rearrange("p (k s) -> p k s", k=DC))\
                    .then_inc(sem("xt_hi"), 1)

            def q(n):
                act.wait_ge(sem("q"), n + 1)
                if n >= 2:
                    act.wait_ge(sem("scores"), 4 * (n - 1))
                copy(qh[:, n % 2, :, :], work_bank("q", n).rearrange("p (c s) -> p c s", c=2), scale=SCALE)\
                    .then_inc(sem("q_hi"), 1)

            def k(n):
                act.wait_ge(sem("k"), n + 1)
                if n >= 2:
                    act.wait_ge(sem("scores"), 4 * (n - 1))
                if n == 0:
                    act.wait_ge(sem("kzero"), 2)
                src = work_bank("k", n).rearrange("p (c s) -> p c s", c=2)
                for h in range(2):
                    rows_ = slice(h * HD, (h + 1) * HD)
                    last = copy(kh[rows_, n % 2, :, h, :], src[rows_, :, :])
                last.then_inc(sem("k_hi"), 1)

            def v_(n):
                b, half, t = n // 4, n % 4 // 2, n % 2
                act.wait_ge(sem("v"), n + 1)
                if n in (0, 1, 4):
                    act.wait_ge(sem("split_lo"), {0: 1, 1: 2, 4: 6}[n])
                if b >= 2:
                    act.wait_ge(sem("pv"), PAIRS * (b - 1))
                copy(v[:, b % 2, t, half * 512:half * 512 + 512], work_bank("v", n)).then_inc(sem("v_sb"), 1)

            def exps(i, qb):
                act.wait_ge(sem("max"), 2 * i + qb + 1)
                if i in (1, 2):
                    act.wait_ge(sem("split_lo"), 3 if i == 1 else 8)
                if i >= 3:
                    act.wait_ge(sem("turn"), 2 * (i - 2))
                for h in range(2):
                    last = act.activation(prob[:, i % 3, qb, h, :], psum[:, qb, h * S:(h + 1) * S], ACT.Exp,
                                          bias=negmax[:, i % 2, qb, h:h + 1],
                                          accum_out=total[:, i % 2, qb, h:h + 1])
                last.then_inc(sem("exp"), 1)

            def turn(i):
                if i in (0, 1):
                    act.wait_ge(sem("split_lo"), 4 if i == 0 else 8)
                for h in range(2):
                    act.wait_ge(sem("turn"), 2 * i + h + 1)
                    if i >= 2:
                        act.wait_ge(sem("pv"), i - 1)
                    copy(probt[:, i % 2, h, :, :], psum[:, 2 + h, :].rearrange("p (k s) -> p k s", k=ST))\
                        .then_inc(sem("probt"), 1)

            def pv(i):
                b, c = divmod(i, PAIRS)
                act.wait_ge(sem("pv"), i + 1)
                if b >= 2:
                    act.wait_ge(sem("o"), ST * (b - 1))
                copy(ah[:, b % 2, c, :], psum[:, 4, 0:S]).then_inc(sem("a_hi"), 1)

            def x2t_(b):
                act.wait_ge(sem("x2t"), b + 1)
                if b >= 1:
                    act.wait_ge(sem("logits"), b)
                copy(x2t[:, :, :], work_bank("x2t", b).rearrange("p (k s) -> p k s", k=DC))\
                    .then_inc(sem("x2t_sb"), 1)

            def gate(b):
                act.wait_ge(sem("shifted"), b + 1)
                act.activation(lexp[:, :, :], logit[:, :, :], ACT.Exp).then_inc(sem("gate_exp"), 1)

            steps = dict(split=split, xt=xt, q=q, k=k, v=v_, turn=turn, pv=pv, x2t=x2t_, gate=gate,
                         scores=lambda i: exps(i, 0), exp1=lambda i: exps(i, 1))
            for stage, n in TIMELINE:
                if stage in steps:
                    steps[stage](n)

            def split_w(e, piece):
                r, part, cut = e % 2, *divmod(piece, WSPLITS // 2)
                act.wait_ge(sem(("w1_in", "w2_in")[part]), 16 * (e + 1))
                if e >= 2:
                    act.wait_ge(sem("down"), ET * (e - 1))
                if e == 1 and piece == 0:
                    act.wait_ge(sem("slots"), B)
                    act.wait_ge(sem("scatter"), 16 * 2 * ST * B)
                    all_stored(act)
                copy(w_piece((w1h, w2h)[part][r], cut), w_piece((w1r, w2r)[part], cut))\
                    .then_inc(sem("wsplit_hi"), 1)

            def turn_rows(e, u):
                at, s0, s1 = TURNS * e + u, 2 * u, min(2 * u + 2, ET)
                act.wait_ge(sem("turn_rows"), at + 1)
                if e >= 2:
                    act.wait_ge(sem("up"), HC * (e - 1))
                src = psum[:, 6 + at % 2, :].rearrange("p (s k c) -> p k s c", k=DC, c=P)
                for kk in range(DC):
                    last = copy(bufh[:, e % 2, kk, s0 * P:s1 * P].rearrange("p (s c) -> p s c", c=P),
                                src[:, kk, 0:s1 - s0, :])
                last.then_inc(sem("buf_hi"), 1)

            act.wait_ge(sem("b1_in"), 16)
            act.wait_ge(sem("q"), STEPS // 2)
            act.wait_ge(sem("k"), STEPS // 2)
            act.wait_ge(sem("v"), 4 * B)
            for piece in range(WSPLITS):
                split_w(0, piece)
            for u in range(TURNS):
                turn_rows(0, u)
            for e in range(NE):
                for j in range(HC):
                    at = HC * e + j
                    act.wait_ge(sem("up"), at + 1)
                    if at >= 2:
                        act.wait_ge(sem("hid_lo"), at - 1)
                    act.activation(hid[:, at % 2, :].rearrange("p (a s) -> p a s", a=2),
                                   psum[:, 2 * (at % 2):2 * (at % 2) + 2, 0:HALF], ACT.Gelu,
                                   bias=b1t[:, e, j:j + 1]).then_inc(sem("gelu"), 1)
                    if e + 1 < NE and j in TURN_AFTER:
                        turn_rows(e + 1, TURN_AFTER.index(j))
                if e + 1 < NE:
                    for piece in range(WSPLITS):
                        split_w(e + 1, piece)

        @block.vector
        def _(dve):
            done = [0]

            def link(ins):
                done[0] += 1
                ins.then_inc(sem("dve"), 1)
                dve.wait_ge(sem("dve"), done[0])

            def work_bank(stage, n):
                return psum[:, 5 + WORKS.index((stage, n)) % WORK_BANKS, :]

            def rest_of(dst, whole, head):
                return dve.tensor_tensor(dst, whole, head.bitcast(F32), ALU.subtract)

            def ln_stats(which, n, src):
                if n >= 1:
                    dve.wait_ge(sem(f"{which}_rstd"), n)
                for t in range(ST):
                    last = dve.bn_stats(stats[:, t, :], src(t))
                link(last)
                for t in range(ST):
                    last = dve.bn_aggr(mean_var[which][:, t, :], stats[:, t, :])
                last.then_inc(sem(f"{which}_var"), 1)

            def ln_apply(which, n, src, dst):
                dve.wait_ge(sem(f"{which}_rstd"), n + 1)
                for t in range(ST):
                    last = dve.tensor_scalar(dst(t), src(t), mean_var[which][:, t, 0:1], rstd[which][:, t:t + 1],
                                             ALU.subtract, ALU.mult)
                last.then_inc(sem(which), 1)

            def split(w):
                dve.wait_ge(sem("split_hi"), w + 1)
                whole, head, rest_ = pieces(w)
                rest_of(rest_, whole, head).then_inc(sem("split_lo"), 1)

            def ln1_stats(b):
                dve.wait_ge(sem(f"x_in{ring3(b)}"), 16 * (b // 3 + 1))
                ln_stats("ln1", b, lambda t: xin[:, ring3(b), t, :])

            def ln1(b):
                if b >= 1:
                    dve.wait_ge(sem("xt"), b)
                ln_apply("ln1", b, lambda t: xin[:, ring3(b), t, :], lambda t: xn[:, t, :])

            def xt(b):
                dve.wait_ge(sem("xt_hi"), b + 1)
                rest_of(xtl[:, b % 2, :, :], work_bank("xt", b).rearrange("p (k s) -> p k s", k=DC),
                        xth[:, b % 2, :, :]).then_inc(sem("xt_lo"), 1)

            def q(n):
                dve.wait_ge(sem("q_hi"), n + 1)
                dve.scalar_tensor_tensor(ql[:, n % 2, :, :], work_bank("q", n).rearrange("p (c s) -> p c s", c=2),
                                         SCALE, qh[:, n % 2, :, :].bitcast(F32), ALU.mult, ALU.subtract)\
                   .then_inc(sem("q_lo"), 1)

            def k(n):
                dve.wait_ge(sem("k_hi"), n + 1)
                if n == 0:
                    dve.wait_ge(sem("kzero_lo"), 2)
                src = work_bank("k", n).rearrange("p (c s) -> p c s", c=2)
                for h in range(2):
                    r = slice(h * HD, (h + 1) * HD)
                    last = rest_of(kl[r, n % 2, :, h, :], src[r, :, :], kh[r, n % 2, :, h, :])
                last.then_inc(sem("k_lo"), 1)

            def scores(i):
                for qb in range(ST):
                    dve.wait_ge(sem("scores"), 2 * i + qb + 1)
                    dve.tensor_reduce(negmax[:, i % 2, qb, :], psum[:, qb, :].rearrange("p (h s) -> p h s", h=2),
                                      AX.X, ALU.max, negate=True).then_inc(sem("max"), 1)

            def norm(i, qb):
                dve.wait_ge(sem("exp"), 2 * i + qb + 1)
                link(dve.reciprocal(invtot[:, i % 2, qb, :], total[:, i % 2, qb, :]))
                for h in range(2):
                    last = dve.tensor_scalar(prob[:, i % 3, qb, h, :], prob[:, i % 3, qb, h, :],
                                             invtot[:, i % 2, qb, h:h + 1], None, ALU.mult)
                last.then_inc(sem("norm"), 1)

            def pv(i):
                b, c = divmod(i, PAIRS)
                dve.wait_ge(sem("a_hi"), i + 1)
                rest_of(al[:, b % 2, c, :], psum[:, 4, 0:S], ah[:, b % 2, c, :]).then_inc(sem("a_lo"), 1)

            def o(n):
                b, t = divmod(n, ST)
                dve.wait_ge(sem("o"), n + 1)
                if t == 0:
                    dve.wait_ge(sem("residual"), ST * (b + 1))
                    if b >= 2:
                        dve.wait_ge(sem(f"x2_out{b % 2}"), 16 * (b // 2))
                dve.tensor_tensor(x2[:, b % 2, t, :], work_bank("o", n)[:, 0:D], xin[:, ring3(b), t, :], ALU.add)\
                   .then_inc(sem("x2"), 1)

            def ln2_stats(b):
                dve.wait_ge(sem("x2"), ST * (b + 1))
                ln_stats("ln2", b, lambda t: x2[:, b % 2, t, :])

            def ln2(b):
                if b >= 2:
                    dve.wait_ge(sem("scatter"), 16 * 2 * ST * (b - 1))
                ln_apply("ln2", b, lambda t: x2[:, b % 2, t, :], lambda t: row[:, b % 2, t, 0:D])

            def logits(b):
                dve.wait_ge(sem("logits"), b + 1)
                if b == 0:
                    dve.wait_ge(sem("const_in"), 48)
                dve.tensor_tensor(logit[:, :, :], work_bank("logits", b)[:, 0:ST * NE]
                                  .rearrange("p (t e) -> p t e", t=ST),
                                  rb_all[:, :].unsqueeze(1).to_broadcast([P, ST, NE]), ALU.add)\
                   .then_inc(sem("biased"), 1)
                dve.wait_ge(sem("biased"), b + 1)
                link(dve.tensor_reduce(lmax[:, :], logit[:, :, :], AX.X, ALU.max))
                dve.tensor_tensor(logit[:, :, :], logit[:, :, :], lmax[:, :].unsqueeze(2).to_broadcast([P, ST, NE]),
                                  ALU.subtract).then_inc(sem("shifted"), 1)

            def gate(b):
                dve.wait_ge(sem("gate_exp"), b + 1)
                link(dve.tensor_reduce(lsum[:, :], lexp[:, :, :], AX.X, ALU.add))
                link(dve.reciprocal(linv[:, :], lsum[:, :]))
                link(dve.tensor_tensor(gates[:, :, :], lexp[:, :, :],
                                       linv[:, :].unsqueeze(2).to_broadcast([P, ST, NE]), ALU.mult))
                shape = [P, ST, NE, NE]
                other = gates[:, :, :].unsqueeze(2).to_broadcast(shape)
                own = gates[:, :, :].unsqueeze(3).to_broadcast(shape)
                for t in range(ST):
                    dve.tensor_tensor(above[:, t], other[:, t], own[:, t], ALU.is_gt)
                    last = dve.tensor_tensor(equal[:, t], other[:, t], own[:, t], ALU.is_equal)
                last.then_inc(sem("compared"), 1)

            def rank_(b):
                shape = [P, ST, NE, NE]
                dve.wait_ge(sem("compared"), b + 1)
                link(dve.tensor_tensor(equal[:, :, :, :], equal[:, :, :, :],
                                       lower[:, :, :].unsqueeze(1).to_broadcast(shape), ALU.mult))
                link(dve.tensor_tensor(above[:, :, :, :], above[:, :, :, :], equal[:, :, :, :], ALU.add))
                link(dve.tensor_reduce(rank[:, :, :], above[:, :, :, :], AX.X, ALU.add))
                dve.tensor_scalar(chosen[:, :, :], rank[:, :, :], 2.0, None, ALU.is_lt).then_inc(sem("chosen"), 1)

            def slot_(b):
                dve.wait_ge(sem("pos"), b + 1)
                count = work_bank("pos", b)[:, 0:ST * NE].rearrange("p (t e) -> p t e", t=ST)
                dve.tensor_tensor(slot[:, :, :], count, slot0[:, :].unsqueeze(1).to_broadcast([P, ST, NE]), ALU.add)
                dve.scalar_tensor_tensor(valid[:, :, :], count, float(CAP), chosen[:, :, :], ALU.is_le, ALU.mult)\
                   .then_inc(sem("slots"), 1)
                dve.wait_ge(sem("slots"), b + 1)
                for t in range(ST):
                    link(dve.tensor_tensor(before[:, :], before[:, :], chosen[:, t, :], ALU.add))
                dve.tensor_tensor(row[:, b % 2, :, GATE:ROW], gates[:, :, :], valid[:, :, :], ALU.mult)
                dve.tensor_scalar(row[:, b % 2, :, ID], tok[:, :], float(b * S), None, ALU.add)
                dve.scalar_tensor_tensor(lowkey[:, :, :], slot[:, :, :], -BIG, valid[:, :, :], ALU.add, ALU.mult)
                dve.scalar_tensor_tensor(highkey[:, :, :], slot[:, :, :], 1.0, valid[:, :, :], ALU.add, ALU.mult)\
                   .then_inc(sem("keys"), 1)

            def pick_(b):
                dve.wait_ge(sem("keys"), b + 1)
                if b >= 2:
                    dve.wait_ge(sem("scatter"), 16 * 2 * ST * (b - 1))
                dve.tensor_reduce(pick[:, 0, :], lowkey[:, :, :], AX.X, ALU.min)
                link(dve.tensor_reduce(pick[:, 1, :], highkey[:, :, :], AX.X, ALU.max))
                dve.tensor_scalar(pick[:, 0, :], pick[:, 0, :], BIG, None, ALU.add)
                link(dve.tensor_scalar(pick[:, 1, :], pick[:, 1, :], -1.0, None, ALU.add))
                link(dve.tensor_tensor(same[:, 0, :], pick[:, 1, :], pick[:, 0, :], ALU.is_le))
                link(dve.scalar_tensor_tensor(pick[:, 1, :], same[:, 0, :], BIG, pick[:, 1, :], ALU.mult, ALU.add))
                dve.tensor_copy(picki[:, b % 2, :, :], pick[:, :, :]).then_inc(sem("picks"), 1)

            dve.memset(kl[HD:P, :, :, 0, :].bitcast(F32), 0.0).then_inc(sem("kzero_lo"), 1)
            dve.memset(kl[0:HD, :, :, 1, :].bitcast(F32), 0.0).then_inc(sem("kzero_lo"), 1)
            steps = dict(split=split, ln1=ln1, xt=xt, q=q, k=k, scores=scores, norm0=lambda i: norm(i, 0),
                         norm1=lambda i: norm(i, 1), pv=pv, o=o, ln1_stats=ln1_stats, ln2_stats=ln2_stats,
                         ln2=ln2, logits=logits, gate=gate, rank=rank_, slot=slot_, pick=pick_)
            for stage, n in TIMELINE:
                if stage in steps:
                    steps[stage](n)

            def split_w(e, piece):
                r, part, cut = e % 2, *divmod(piece, WSPLITS // 2)
                dve.wait_ge(sem("wsplit_hi"), WSPLITS * e + piece + 1)
                rest_of(w_piece((w1l, w2l)[part][r], cut), w_piece((w1r, w2r)[part], cut),
                        w_piece((w1h, w2h)[part][r], cut)).then_inc(sem("wsplit_lo"), 1)

            def turn_rows(e, u):
                at, s0, s1 = TURNS * e + u, 2 * u, min(2 * u + 2, ET)
                dve.wait_ge(sem("buf_hi"), at + 1)
                src = psum[:, 6 + at % 2, :].rearrange("p (s k c) -> p k s c", k=DC, c=P)
                for kk in range(DC):
                    part = lambda a: a[:, e % 2, kk, s0 * P:s1 * P].rearrange("p (s c) -> p s c", c=P)
                    last = rest_of(part(bufl), src[:, kk, 0:s1 - s0, :], part(bufh))
                last.then_inc(sem("buf_lo"), 1)

            def row_numbers(e):
                dve.wait_ge(sem(f"rows_in{e % 2}"), 16 * (e // 2 + 1))
                if e >= 2:
                    dve.wait_ge(sem("added"), 16 * ET * (e - 1))
                dve.tensor_copy(rowi[:, e % 2, :], rows[:, e % 2, :, ID]).then_inc(sem("rowi"), 1)

            def split_hid(at):
                j = at % HC
                dve.wait_ge(sem("gelu"), at + 1)
                if j == 0 and at:
                    dve.wait_ge(sem("down"), ET * (at // HC))
                dve.tensor_copy(hidh[:, j, :], hid[:, at % 2, :]).then_inc(sem("hid_hi"), 1)
                dve.wait_ge(sem("hid_hi"), at + 1)
                rest_of(hidl[:, j, :], hid[:, at % 2, :], hidh[:, j, :]).then_inc(sem("hid_lo"), 1)

            def weigh(e, s):
                dve.wait_ge(sem("down"), ET * e + s + 1)
                if e >= 2 and s == 0:
                    dve.wait_ge(sem("added"), 16 * ET * (e - 1))
                link(dve.tensor_tensor(y[:, e % 2, s, :], psum[:, 4 + (ET * e + s) % 2, 0:D], b2_all[:, e, :], ALU.add))
                dve.tensor_scalar(y[:, e % 2, s, :], y[:, e % 2, s, :], rows[:, e % 2, s, GATE + e:GATE + e + 1],
                                  None, ALU.mult).then_inc(sem("y"), 1)

            for piece in range(WSPLITS):
                split_w(0, piece)
            for u in range(TURNS):
                turn_rows(0, u)
            for e in range(NE):
                for j in range(HC):
                    split_hid(HC * e + j)
                    if e + 1 < NE and j in TURN_AFTER:
                        turn_rows(e + 1, TURN_AFTER.index(j))
                row_numbers(e)
                if e == 0:
                    dve.wait_ge(sem("b2_in"), 16)
                for s in range(ET):
                    if e + 1 < NE and s < WSPLITS:
                        split_w(e + 1, s)
                    weigh(e, s)


def kernel(x, ctx_768, L0_xattn_w_q, L0_xattn_w_k, L0_xattn_w_v, L0_xattn_w_o, L0_xattn_b_o,
           L0_ffn_router_w, L0_ffn_router_b, L0_ffn_w1, L0_ffn_b1, L0_ffn_w2, L0_ffn_b2):
    import numpy as np
    import concourse.bacc as bacc
    from concourse.bass_utils import run_bass_kernel_spmd as run

    ins = {
        "x": x,
        "ctxt": np.asarray(ctx_768).reshape(N, CD).T,
        "wq": L0_xattn_w_q, "wk": L0_xattn_w_k, "wv": L0_xattn_w_v, "wo": L0_xattn_w_o, "bo": L0_xattn_b_o,
        "rw": L0_ffn_router_w, "rb": L0_ffn_router_b, "w1": L0_ffn_w1,
        "b1": np.asarray(L0_ffn_b1).reshape(NE, HC, P).transpose(2, 0, 1),
        "w2": L0_ffn_w2, "b2": L0_ffn_b2,
    }
    nc = bacc.Bacc("TRN2", target_bir_lowering=False, num_devices=1)
    arrays, args = {}, []
    for name, a in ins.items():
        a = np.ascontiguousarray(a)
        arrays[f"in_{name}"] = a
        args.append(nc.dram_tensor(f"in_{name}", a.shape, F32, kind="ExternalInput").ap())
    args.append(nc.dram_tensor("out_rows", (N + CAP, D), F32, kind="ExternalOutput").ap())
    build(nc, *args)
    r = run(nc, [arrays], core_ids=[0])
    return r.results[0]["out_rows"][:N].reshape(B, S, D)
```
